# Optimizing a Trainium2 kernel written in Bass

```python
import numpy as np
import jax
import jax.numpy as jnp

def _softmax(x, axis=-1):
    return jax.nn.softmax(x, axis=axis)

def _gelu(x):
    return jax.nn.gelu(x, approximate=True)

def _silu(x):
    return jax.nn.silu(x)

def _sigmoid(x):
    return jax.nn.sigmoid(x)

def _layernorm(x, axis=-1, eps=1e-05):
    m = jnp.mean(x, axis=axis, keepdims=True)
    v = jnp.var(x, axis=axis, keepdims=True)
    return (x - m) / jnp.sqrt(v + eps)

def _scatter_add(tgt, idx, src, axis=0):
    return tgt.at[idx].add(src)

def _segment_sum(src, seg, n):
    return jax.ops.segment_sum(src, seg, n)
kernel_name = 'mk_lm_tower_d2_tok_ids768_r4_3ac4ac'

def setup_inputs(seed: int=0):
    np.random.seed(seed)
    _w = jnp.asarray

    def _rec_inputs():
        import jax
        import jax.numpy as jnp
        _rk = jax.random.key(seed)
        x = jax.random.randint(jax.random.fold_in(_rk, 1), (128, 128), 0, 31921, jnp.int32)
        return x
    x = _rec_inputs()

    def _L0_tok_setup():
        import jax, jax.numpy as jnp
        import numpy as np
        B, L, V, D_MODEL = (1, 512, 8000, 192)
        N_LAYER, D_STATE, EXPAND, D_CONV = (2, 16, 2, 4)
        D_INNER = EXPAND * D_MODEL
        DT_RANK = -(-D_MODEL // D_STATE)
        EPS = 1e-05

        def _rmsnorm(x, w):
            return x * jax.lax.rsqrt(jnp.mean(x * x, axis=-1, keepdims=True) + EPS) * w

        def _selective_scan(u, delta, A, Bm, Cm, D):
            deltaA = jnp.exp(delta[..., None] * A)
            dBu = delta[..., None] * Bm[:, :, None, :] * u[..., None]

            def comb(c1, c2):
                a1, b1 = c1
                a2, b2 = c2
                return (a2 * a1, a2 * b1 + b2)
            _, h = jax.lax.associative_scan(comb, (deltaA, dBu), axis=1)
            y = jnp.einsum('bldn,bln->bld', h, Cm)
            return y + u * D

        def _mamba_block(x, in_proj_w, conv_w, conv_b, x_proj_w, dt_proj_w, dt_proj_b, A_log, D, out_proj_w):
            xz = x @ in_proj_w
            xr, res = jnp.split(xz, 2, axis=-1)
            xc = jax.lax.conv_general_dilated(jnp.swapaxes(xr, 1, 2), conv_w, (1,), [(D_CONV - 1, 0)], feature_group_count=D_INNER, dimension_numbers=('NCH', 'OIH', 'NCH'))
            xr = jax.nn.silu(jnp.swapaxes(xc + conv_b[:, None], 1, 2))
            A = -jnp.exp(A_log)
            x_dbl = xr @ x_proj_w
            dt, Bm, Cm = jnp.split(x_dbl, [DT_RANK, DT_RANK + D_STATE], axis=-1)
            delta = jax.nn.softplus(dt @ dt_proj_w + dt_proj_b)
            y = _selective_scan(xr, delta, A, Bm, Cm, D)
            return y * jax.nn.silu(res) @ out_proj_w
        key = jax.random.key(seed)
        ks = jax.random.split(key, 12)
        s = 0.02
        inp = {'input_ids': jax.random.randint(ks[0], (B, L), 0, V), 'emb': jax.random.normal(ks[1], (V, D_MODEL), jnp.float32) * s, 'norm_w': jnp.ones((N_LAYER, D_MODEL), jnp.float32), 'in_proj_w': jax.random.normal(ks[2], (N_LAYER, D_MODEL, 2 * D_INNER), jnp.float32) * s, 'conv_w': jax.random.normal(ks[3], (N_LAYER, D_INNER, 1, D_CONV), jnp.float32) * s, 'conv_b': jnp.zeros((N_LAYER, D_INNER), jnp.float32), 'x_proj_w': jax.random.normal(ks[4], (N_LAYER, D_INNER, DT_RANK + 2 * D_STATE), jnp.float32) * s, 'dt_proj_w': jax.random.normal(ks[5], (N_LAYER, DT_RANK, D_INNER), jnp.float32) * s, 'dt_proj_b': jax.random.normal(ks[6], (N_LAYER, D_INNER), jnp.float32) * s, 'A_log': jnp.tile(jnp.log(jnp.arange(1, D_STATE + 1, dtype=jnp.float32)), (N_LAYER, D_INNER, 1)), 'D': jnp.ones((N_LAYER, D_INNER), jnp.float32), 'out_proj_w': jax.random.normal(ks[7], (N_LAYER, D_INNER, D_MODEL), jnp.float32) * s}
        return inp
    _L0_tok_all = _L0_tok_setup()
    _L0_tok_in = {k: v for k, v in _L0_tok_all.items() if k in ('emb', 'norm_w', 'in_proj_w', 'conv_w', 'conv_b', 'x_proj_w', 'dt_proj_w', 'dt_proj_b', 'A_log', 'D', 'out_proj_w')}
    del _L0_tok_all

    def _L0_attn_setup():
        import jax, jax.numpy as jnp
        import numpy as np
        from jax import lax

        def _silu(v):
            return v * jax.nn.sigmoid(v)
        key = jax.random.key(seed)
        ks = jax.random.split(key, 8)
        b, l, d_model = (2, 256, 192)
        expand, d_state, d_conv = (2, 16, 4)
        d_inner = d_model * expand
        dt_rank = -(-d_model // 16)
        x = jax.random.normal(ks[0], (b, l, d_model), jnp.float32)
        W_in = jax.random.normal(ks[1], (d_model, 2 * d_inner), jnp.float32) * 0.02
        conv_w = jax.random.normal(ks[2], (d_inner, 1, d_conv), jnp.float32) * 0.1
        conv_b = jnp.zeros((d_inner,), jnp.float32)
        W_x = jax.random.normal(ks[3], (d_inner, dt_rank + 2 * d_state), jnp.float32) * 0.02
        W_dt = jax.random.normal(ks[4], (dt_rank, d_inner), jnp.float32) * 0.02
        b_dt = jax.random.normal(ks[5], (d_inner,), jnp.float32) * 0.02
        A_log = jnp.broadcast_to(jnp.log(jnp.arange(1, d_state + 1, dtype=jnp.float32)), (d_inner, d_state)).copy()
        D = jnp.ones((d_inner,), jnp.float32)
        W_out = jax.random.normal(ks[6], (d_inner, d_model), jnp.float32) * 0.02
        return {'x': x, 'W_in': W_in, 'conv_w': conv_w, 'conv_b': conv_b, 'W_x': W_x, 'W_dt': W_dt, 'b_dt': b_dt, 'A_log': A_log, 'D': D, 'W_out': W_out}
    _L0_attn_all = _L0_attn_setup()
    _L0_attn_in = {k: v for k, v in _L0_attn_all.items() if k in ('W_in', 'conv_w', 'conv_b', 'W_x', 'W_dt', 'b_dt', 'A_log', 'D', 'W_out')}
    del _L0_attn_all

    def _L0_ffn_setup():
        import jax, jax.numpy as jnp
        import numpy as np
        import math
        B, T, C = (8, 512, 192)
        E = 3
        HD = C // E
        TOPK = 2
        NGLOB = 4

        def _masked_softmax(att, mask):
            att = jnp.where(mask, -jnp.inf, att)
            return jax.nn.softmax(att, axis=-1)
        key = jax.random.key(seed)
        ks = jax.random.split(key, 16)
        s = 0.02
        return {'x': jax.random.normal(ks[0], (B, T, C), jnp.float32), 'Wqk': jax.random.normal(ks[1], (C, 2 * C), jnp.float32) * s, 'bqk': jnp.zeros((2 * C,), jnp.float32), 'Wv': jax.random.normal(ks[2], (E, C, HD), jnp.float32) * s, 'bv': jnp.zeros((E, HD), jnp.float32), 'conv_w': jax.random.normal(ks[3], (HD, 1, 3), jnp.float32) * s, 'conv_b': jnp.zeros((HD,), jnp.float32), 'glob': jax.random.normal(ks[4], (NGLOB, HD), jnp.float32) * 0.02, 'pos_bias': jnp.zeros((64, 64), jnp.float32), 'Wg1': jax.random.normal(ks[5], (C, 32), jnp.float32) * s, 'bg1': jnp.zeros((32,), jnp.float32), 'Wg2': jax.random.normal(ks[6], (32, E), jnp.float32) * s, 'bg2': jnp.zeros((E,), jnp.float32), 'Wp': jax.random.normal(ks[7], (C, C), jnp.float32) * s, 'bp': jnp.zeros((C,), jnp.float32)}
    _L0_ffn_all = _L0_ffn_setup()
    _L0_ffn_in = {k: v for k, v in _L0_ffn_all.items() if k in ('Wqk', 'bqk', 'Wv', 'bv', 'conv_w', 'conv_b', 'glob', 'pos_bias', 'Wg1', 'bg1', 'Wg2', 'bg2', 'Wp', 'bp')}
    del _L0_ffn_all

    def _L1_attn_setup():
        import jax, jax.numpy as jnp
        import numpy as np
        H = 12
        W = 128
        G = 32
        NEG = -1000000000.0

        def _longformer_attn(hidden, Wq, bq, Wk, bk, Wv, bv, Wo, bo):
            B, S, D = hidden.shape
            dh = D // H
            scale = jnp.asarray(dh, hidden.dtype) ** (-0.5)

            def proj(Wm, bm):
                return (hidden @ Wm + bm).reshape(B, S, H, dh).transpose(0, 2, 1, 3)
            q = proj(Wq, bq) * scale
            k = proj(Wk, bk)
            v = proj(Wv, bv)
            nc = S // W
            q_ch = q.reshape(B, H, nc, W, dh)
            kp = jnp.pad(k, ((0, 0), (0, 0), (W, W), (0, 0)))
            vp = jnp.pad(v, ((0, 0), (0, 0), (W, W), (0, 0)))
            idx = (jnp.arange(nc) * W)[:, None] + jnp.arange(3 * W)[None, :]
            k_ch = kp[:, :, idx]
            v_ch = vp[:, :, idx]
            band = jnp.einsum('bhcqd,bhckd->bhcqk', q_ch, k_ch)
            qi = jnp.arange(W)[:, None]
            kj = jnp.arange(3 * W)[None, :]
            in_band = (kj >= qi) & (kj <= qi + 2 * W)
            j = (jnp.arange(nc) * W)[:, None, None] + kj[None] - W
            valid = in_band[None] & (j >= G) & (j < S)
            band = jnp.where(valid[None, None], band, NEG)
            band = band.reshape(B, H, S, 3 * W)
            gsc = jnp.einsum('bhsd,bhgd->bhsg', q, k[:, :, :G])
            scores = jnp.concatenate([gsc, band], axis=-1)
            probs = jax.nn.softmax(scores, axis=-1)
            out = jnp.einsum('bhsg,bhgd->bhsd', probs[..., :G], v[:, :, :G])
            pb = probs[..., G:].reshape(B, H, nc, W, 3 * W)
            out = out + jnp.einsum('bhcqk,bhckd->bhcqd', pb, v_ch).reshape(B, H, S, dh)
            gq_probs = jax.nn.softmax(jnp.einsum('bhgd,bhsd->bhgs', q[:, :, :G], k), axis=-1)
            out_g = jnp.einsum('bhgs,bhsd->bhgd', gq_probs, v)
            out = out.at[:, :, :G].set(out_g)
            out = out.transpose(0, 2, 1, 3).reshape(B, S, D)
            return out @ Wo + bo
        key = jax.random.key(seed)
        ks = jax.random.split(key, 9)
        B, S, D = (1, 1024, 192)
        std = 0.02
        f32 = jnp.float32
        return {'hidden_states': jax.random.normal(ks[0], (B, S, D), f32), 'Wq': jax.random.normal(ks[1], (D, D), f32) * std, 'bq': jnp.zeros((D,), f32), 'Wk': jax.random.normal(ks[2], (D, D), f32) * std, 'bk': jnp.zeros((D,), f32), 'Wv': jax.random.normal(ks[3], (D, D), f32) * std, 'bv': jnp.zeros((D,), f32), 'Wo': jax.random.normal(ks[4], (D, D), f32) * std, 'bo': jnp.zeros((D,), f32)}
    _L1_attn_all = _L1_attn_setup()
    _L1_attn_in = {k: v for k, v in _L1_attn_all.items() if k in ('Wq', 'bq', 'Wk', 'bk', 'Wv', 'bv', 'Wo', 'bo')}
    del _L1_attn_all

    def _L1_ffn_setup():
        import jax, jax.numpy as jnp
        import numpy as np
        B, S, D_IN, D_HID, D_OUT = (32, 128, 192, 768, 192)
        key = jax.random.key(seed)
        k1, k2, k3, k4 = jax.random.split(key, 4)
        init_k = float(np.sqrt(1.0 / D_IN))
        init_k2 = float(np.sqrt(1.0 / D_HID))
        x = jax.random.normal(k1, (B, S, D_IN), dtype=jnp.float32)
        in_weight = jax.random.uniform(k2, (D_HID, D_IN), dtype=jnp.float32, minval=-init_k, maxval=init_k)
        in_bias = jax.random.uniform(k3, (D_HID,), dtype=jnp.float32, minval=-init_k, maxval=init_k)
        out_weight = jax.random.uniform(k4, (D_HID, D_OUT), dtype=jnp.float32, minval=-init_k2, maxval=init_k2)
        return {'x': x, 'in_weight': in_weight, 'in_bias': in_bias, 'out_weight': out_weight}
    _L1_ffn_all = _L1_ffn_setup()
    _L1_ffn_in = {k: v for k, v in _L1_ffn_all.items() if k in ('in_weight', 'in_bias', 'out_weight')}
    del _L1_ffn_all
    return {'x': x, 'L0_tok_emb': _L0_tok_in['emb'], 'L0_tok_norm_w': _L0_tok_in['norm_w'], 'L0_tok_in_proj_w': _L0_tok_in['in_proj_w'], 'L0_tok_conv_w': _L0_tok_in['conv_w'], 'L0_tok_conv_b': _L0_tok_in['conv_b'], 'L0_tok_x_proj_w': _L0_tok_in['x_proj_w'], 'L0_tok_dt_proj_w': _L0_tok_in['dt_proj_w'], 'L0_tok_dt_proj_b': _L0_tok_in['dt_proj_b'], 'L0_tok_A_log': _L0_tok_in['A_log'], 'L0_tok_D': _L0_tok_in['D'], 'L0_tok_out_proj_w': _L0_tok_in['out_proj_w'], 'L0_attn_W_in': _L0_attn_in['W_in'], 'L0_attn_conv_w': _L0_attn_in['conv_w'], 'L0_attn_conv_b': _L0_attn_in['conv_b'], 'L0_attn_W_x': _L0_attn_in['W_x'], 'L0_attn_W_dt': _L0_attn_in['W_dt'], 'L0_attn_b_dt': _L0_attn_in['b_dt'], 'L0_attn_A_log': _L0_attn_in['A_log'], 'L0_attn_D': _L0_attn_in['D'], 'L0_attn_W_out': _L0_attn_in['W_out'], 'L0_ffn_Wqk': _L0_ffn_in['Wqk'], 'L0_ffn_bqk': _L0_ffn_in['bqk'], 'L0_ffn_Wv': _L0_ffn_in['Wv'], 'L0_ffn_bv': _L0_ffn_in['bv'], 'L0_ffn_conv_w': _L0_ffn_in['conv_w'], 'L0_ffn_conv_b': _L0_ffn_in['conv_b'], 'L0_ffn_glob': _L0_ffn_in['glob'], 'L0_ffn_pos_bias': _L0_ffn_in['pos_bias'], 'L0_ffn_Wg1': _L0_ffn_in['Wg1'], 'L0_ffn_bg1': _L0_ffn_in['bg1'], 'L0_ffn_Wg2': _L0_ffn_in['Wg2'], 'L0_ffn_bg2': _L0_ffn_in['bg2'], 'L0_ffn_Wp': _L0_ffn_in['Wp'], 'L0_ffn_bp': _L0_ffn_in['bp'], 'L1_attn_Wq': _L1_attn_in['Wq'], 'L1_attn_bq': _L1_attn_in['bq'], 'L1_attn_Wk': _L1_attn_in['Wk'], 'L1_attn_bk': _L1_attn_in['bk'], 'L1_attn_Wv': _L1_attn_in['Wv'], 'L1_attn_bv': _L1_attn_in['bv'], 'L1_attn_Wo': _L1_attn_in['Wo'], 'L1_attn_bo': _L1_attn_in['bo'], 'L1_ffn_in_weight': _L1_ffn_in['in_weight'], 'L1_ffn_in_bias': _L1_ffn_in['in_bias'], 'L1_ffn_out_weight': _L1_ffn_in['out_weight']}

def reference(x, L0_tok_emb, L0_tok_norm_w, L0_tok_in_proj_w, L0_tok_conv_w, L0_tok_conv_b, L0_tok_x_proj_w, L0_tok_dt_proj_w, L0_tok_dt_proj_b, L0_tok_A_log, L0_tok_D, L0_tok_out_proj_w, L0_attn_W_in, L0_attn_conv_w, L0_attn_conv_b, L0_attn_W_x, L0_attn_W_dt, L0_attn_b_dt, L0_attn_A_log, L0_attn_D, L0_attn_W_out, L0_ffn_Wqk, L0_ffn_bqk, L0_ffn_Wv, L0_ffn_bv, L0_ffn_conv_w, L0_ffn_conv_b, L0_ffn_glob, L0_ffn_pos_bias, L0_ffn_Wg1, L0_ffn_bg1, L0_ffn_Wg2, L0_ffn_bg2, L0_ffn_Wp, L0_ffn_bp, L1_attn_Wq, L1_attn_bq, L1_attn_Wk, L1_attn_bk, L1_attn_Wv, L1_attn_bv, L1_attn_Wo, L1_attn_bo, L1_ffn_in_weight, L1_ffn_in_bias, L1_ffn_out_weight):
    import jax
    import jax.numpy as jnp

    def _L0_tok_ref(input_ids, emb, norm_w, in_proj_w, conv_w, conv_b, x_proj_w, dt_proj_w, dt_proj_b, A_log, D, out_proj_w):
        import jax, jax.numpy as jnp
        import numpy as np
        B, L, V, D_MODEL = (1, 512, 8000, 192)
        N_LAYER, D_STATE, EXPAND, D_CONV = (2, 16, 2, 4)
        D_INNER = EXPAND * D_MODEL
        DT_RANK = -(-D_MODEL // D_STATE)
        EPS = 1e-05

        def _rmsnorm(x, w):
            return x * jax.lax.rsqrt(jnp.mean(x * x, axis=-1, keepdims=True) + EPS) * w

        def _selective_scan(u, delta, A, Bm, Cm, D):
            deltaA = jnp.exp(delta[..., None] * A)
            dBu = delta[..., None] * Bm[:, :, None, :] * u[..., None]

            def comb(c1, c2):
                a1, b1 = c1
                a2, b2 = c2
                return (a2 * a1, a2 * b1 + b2)
            _, h = jax.lax.associative_scan(comb, (deltaA, dBu), axis=1)
            y = jnp.einsum('bldn,bln->bld', h, Cm)
            return y + u * D

        def _mamba_block(x, in_proj_w, conv_w, conv_b, x_proj_w, dt_proj_w, dt_proj_b, A_log, D, out_proj_w):
            xz = x @ in_proj_w
            xr, res = jnp.split(xz, 2, axis=-1)
            xc = jax.lax.conv_general_dilated(jnp.swapaxes(xr, 1, 2), conv_w, (1,), [(D_CONV - 1, 0)], feature_group_count=D_INNER, dimension_numbers=('NCH', 'OIH', 'NCH'))
            xr = jax.nn.silu(jnp.swapaxes(xc + conv_b[:, None], 1, 2))
            A = -jnp.exp(A_log)
            x_dbl = xr @ x_proj_w
            dt, Bm, Cm = jnp.split(x_dbl, [DT_RANK, DT_RANK + D_STATE], axis=-1)
            delta = jax.nn.softplus(dt @ dt_proj_w + dt_proj_b)
            y = _selective_scan(xr, delta, A, Bm, Cm, D)
            return y * jax.nn.silu(res) @ out_proj_w
        x = emb[input_ids]
        for i in range(N_LAYER):
            x = x + _mamba_block(_rmsnorm(x, norm_w[i]), in_proj_w[i], conv_w[i], conv_b[i], x_proj_w[i], dt_proj_w[i], dt_proj_b[i], A_log[i], D[i], out_proj_w[i])
        return x

    def _L0_attn_ref(x, W_in, conv_w, conv_b, W_x, W_dt, b_dt, A_log, D, W_out):
        import jax, jax.numpy as jnp
        import numpy as np
        from jax import lax

        def _silu(v):
            return v * jax.nn.sigmoid(v)
        b, l, d_model = x.shape
        d_inner, _, d_conv = conv_w.shape
        dt_rank = W_dt.shape[0]
        n = A_log.shape[1]
        x_and_res = x @ W_in
        xi, res = jnp.split(x_and_res, 2, axis=-1)
        xc = jnp.transpose(xi, (0, 2, 1))
        xc = lax.conv_general_dilated(xc, conv_w, window_strides=(1,), padding=[(d_conv - 1, 0)], dimension_numbers=('NCH', 'OIH', 'NCH'), feature_group_count=d_inner)
        xc = xc + conv_b[None, :, None]
        u = _silu(jnp.transpose(xc, (0, 2, 1)))
        A = -jnp.exp(A_log.astype(jnp.float32))
        x_dbl = u @ W_x
        delta = x_dbl[..., :dt_rank]
        B = x_dbl[..., dt_rank:dt_rank + n]
        C = x_dbl[..., dt_rank + n:]
        delta = jax.nn.softplus(delta @ W_dt + b_dt)
        deltaA = jnp.exp(delta[..., None] * A)
        deltaB_u = delta[..., None] * B[:, :, None, :] * u[..., None]

        def combine(c1, c2):
            a1, b1 = c1
            a2, b2 = c2
            return (a1 * a2, a2 * b1 + b2)
        _, hs = lax.associative_scan(combine, (deltaA, deltaB_u), axis=1)
        y = jnp.einsum('bldn,bln->bld', hs, C) + u * D
        y = y * _silu(res)
        out = y @ W_out
        return out

    def _L0_ffn_ref(x, Wqk, bqk, Wv, bv, conv_w, conv_b, glob, pos_bias, Wg1, bg1, Wg2, bg2, Wp, bp):
        import jax, jax.numpy as jnp
        import numpy as np
        import math
        B, T, C = (8, 512, 192)
        E = 3
        HD = C // E
        TOPK = 2
        NGLOB = 4

        def _masked_softmax(att, mask):
            att = jnp.where(mask, -jnp.inf, att)
            return jax.nn.softmax(att, axis=-1)
        Bx, Tx, Cx = x.shape
        scale = 1.0 / math.sqrt(HD)
        gate = jax.nn.softmax(jax.nn.relu(x @ Wg1 + bg1) @ Wg2 + bg2, axis=-1)
        top_w, top_i = jax.lax.top_k(gate, TOPK)
        top_w = jax.nn.softmax(top_w, axis=-1)
        qk = x @ Wqk + bqk
        q, k = (qk[..., :Cx], qk[..., Cx:])
        q = q.reshape(Bx, Tx, E, HD)
        k = k.reshape(Bx, Tx, E, HD)
        rows = jnp.arange(Tx)[:, None]
        ys = []
        for e in range(E):
            qe = q[:, :, e]
            ke = k[:, :, e]
            ve = x @ Wv[e] + bv[e]
            if e == 0:
                qc = jnp.transpose(qe, (0, 2, 1))
                qc = jax.lax.conv_general_dilated(qc, conv_w, window_strides=(1,), padding=((1, 1),), feature_group_count=HD, dimension_numbers=('NCH', 'OIH', 'NCH'))
                qe = jnp.transpose(qc + conv_b[None, :, None], (0, 2, 1))
            elif e == 1:
                gb = jnp.broadcast_to(glob[None], (Bx, NGLOB, HD))
                ke = jnp.concatenate([ke, gb], axis=1)
                ve = jnp.concatenate([ve, gb], axis=1)
            att = jnp.einsum('btd,bsd->bts', qe, ke) * scale
            if e == 2 and Tx <= 64:
                att = att + pos_bias[:Tx, :Tx][None]
            S = att.shape[-1]
            mask = jnp.arange(S)[None, :] > rows
            att = _masked_softmax(att, mask[None])
            ys.append(jnp.einsum('bts,bsd->btd', att, ve))
        ys = jnp.stack(ys, axis=2)
        w_e = jnp.sum(jax.nn.one_hot(top_i, E, dtype=x.dtype) * top_w[..., None], axis=-2)
        combined = (ys * w_e[..., None]).reshape(Bx, Tx, Cx)
        return combined @ Wp + bp

    def _L1_attn_ref(hidden_states, Wq, bq, Wk, bk, Wv, bv, Wo, bo):
        import jax, jax.numpy as jnp
        import numpy as np
        H = 12
        W = 128
        G = 32
        NEG = -1000000000.0

        def _longformer_attn(hidden, Wq, bq, Wk, bk, Wv, bv, Wo, bo):
            B, S, D = hidden.shape
            dh = D // H
            scale = jnp.asarray(dh, hidden.dtype) ** (-0.5)

            def proj(Wm, bm):
                return (hidden @ Wm + bm).reshape(B, S, H, dh).transpose(0, 2, 1, 3)
            q = proj(Wq, bq) * scale
            k = proj(Wk, bk)
            v = proj(Wv, bv)
            nc = S // W
            q_ch = q.reshape(B, H, nc, W, dh)
            kp = jnp.pad(k, ((0, 0), (0, 0), (W, W), (0, 0)))
            vp = jnp.pad(v, ((0, 0), (0, 0), (W, W), (0, 0)))
            idx = (jnp.arange(nc) * W)[:, None] + jnp.arange(3 * W)[None, :]
            k_ch = kp[:, :, idx]
            v_ch = vp[:, :, idx]
            band = jnp.einsum('bhcqd,bhckd->bhcqk', q_ch, k_ch)
            qi = jnp.arange(W)[:, None]
            kj = jnp.arange(3 * W)[None, :]
            in_band = (kj >= qi) & (kj <= qi + 2 * W)
            j = (jnp.arange(nc) * W)[:, None, None] + kj[None] - W
            valid = in_band[None] & (j >= G) & (j < S)
            band = jnp.where(valid[None, None], band, NEG)
            band = band.reshape(B, H, S, 3 * W)
            gsc = jnp.einsum('bhsd,bhgd->bhsg', q, k[:, :, :G])
            scores = jnp.concatenate([gsc, band], axis=-1)
            probs = jax.nn.softmax(scores, axis=-1)
            out = jnp.einsum('bhsg,bhgd->bhsd', probs[..., :G], v[:, :, :G])
            pb = probs[..., G:].reshape(B, H, nc, W, 3 * W)
            out = out + jnp.einsum('bhcqk,bhckd->bhcqd', pb, v_ch).reshape(B, H, S, dh)
            gq_probs = jax.nn.softmax(jnp.einsum('bhgd,bhsd->bhgs', q[:, :, :G], k), axis=-1)
            out_g = jnp.einsum('bhgs,bhsd->bhgd', gq_probs, v)
            out = out.at[:, :, :G].set(out_g)
            out = out.transpose(0, 2, 1, 3).reshape(B, S, D)
            return out @ Wo + bo
        return _longformer_attn(hidden_states, Wq, bq, Wk, bk, Wv, bv, Wo, bo)

    def _L1_ffn_ref(x, in_weight, in_bias, out_weight):
        import jax, jax.numpy as jnp
        import numpy as np
        B, S, D_IN, D_HID, D_OUT = (32, 128, 192, 768, 192)
        lead = x.shape[:-1]
        xt = x.reshape(-1, in_weight.shape[1])
        h = jax.nn.gelu(jnp.einsum('td,hd->th', xt, in_weight) + in_bias, approximate=False)
        out = jnp.einsum('th,ho->to', h, out_weight)
        return out.reshape(*lead, out_weight.shape[1])
    h = _L0_tok_ref(x, L0_tok_emb, L0_tok_norm_w, L0_tok_in_proj_w, L0_tok_conv_w, L0_tok_conv_b, L0_tok_x_proj_w, L0_tok_dt_proj_w, L0_tok_dt_proj_b, L0_tok_A_log, L0_tok_D, L0_tok_out_proj_w)
    h = h + _L0_attn_ref(_layernorm(h, axis=-1), L0_attn_W_in, L0_attn_conv_w, L0_attn_conv_b, L0_attn_W_x, L0_attn_W_dt, L0_attn_b_dt, L0_attn_A_log, L0_attn_D, L0_attn_W_out)
    h = h + _L0_ffn_ref(_layernorm(h, axis=-1), L0_ffn_Wqk, L0_ffn_bqk, L0_ffn_Wv, L0_ffn_bv, L0_ffn_conv_w, L0_ffn_conv_b, L0_ffn_glob, L0_ffn_pos_bias, L0_ffn_Wg1, L0_ffn_bg1, L0_ffn_Wg2, L0_ffn_bg2, L0_ffn_Wp, L0_ffn_bp)
    h = h + _L1_attn_ref(_layernorm(h, axis=-1), L1_attn_Wq, L1_attn_bq, L1_attn_Wk, L1_attn_bk, L1_attn_Wv, L1_attn_bv, L1_attn_Wo, L1_attn_bo)
    h = h + _L1_ffn_ref(_layernorm(h, axis=-1), L1_ffn_in_weight, L1_ffn_in_bias, L1_ffn_out_weight)
    return h

_drawn_inputs = setup_inputs


def setup_inputs(seed=0):
    import zlib

    import numpy as np

    out = dict(_drawn_inputs(seed))
    spreads = {'L0_tok_norm_w': (1.0, 0.6),
     'L0_tok_conv_b': (0.0, 0.1),
     'L0_tok_D': (1.0, 0.6),
     'L0_attn_conv_b': (0.0, 0.1),
     'L0_attn_D': (1.0, 0.6),
     'L0_ffn_bqk': (0.0, 0.8),
     'L0_ffn_bv': (0.0, 0.1),
     'L0_ffn_conv_b': (0.0, 2.0),
     'L0_ffn_pos_bias': (0.0, 0.1),
     'L0_ffn_bg1': (0.0, 0.8),
     'L0_ffn_bg2': (0.0, 0.351),
     'L0_ffn_bp': (0.0, 0.1),
     'L1_attn_bq': (0.0, 0.8),
     'L1_attn_bk': (0.0, 2.0),
     'L1_attn_bv': (0.0, 0.1),
     'L1_attn_bo': (0.0, 0.1)}
    factors = {'L0_tok_conv_w': 8.0,
     'L0_tok_x_proj_w': 8.0,
     'L0_tok_dt_proj_w': 52.518,
     'L0_tok_dt_proj_b': 64.0,
     'L0_tok_A_log': 64.0,
     'L0_attn_conv_w': 4.296,
     'L0_attn_W_x': 8.0,
     'L0_attn_W_dt': 47.028,
     'L0_attn_b_dt': 48.787,
     'L0_attn_A_log': 36.105,
     'L0_ffn_Wqk': 8.0,
     'L0_ffn_conv_w': 30.795,
     'L0_ffn_Wg1': 8.0,
     'L0_ffn_Wg2': 8.0,
     'L1_attn_Wq': 8.0,
     'L1_attn_Wk': 8.0}
    for name, (base, spread) in spreads.items():
        noise = np.random.default_rng([zlib.crc32(name.encode()), seed]).standard_normal(out[name].shape)
        drawn = base * np.exp(spread * noise) if base else spread * noise
        out[name] = jnp.asarray(drawn.astype(out[name].dtype))
    for name, factor in factors.items():
        out[name] = (out[name] * factor).astype(out[name].dtype)
    return out
```

```python
from contextlib import ExitStack

import concourse.bass as bass
from concourse import mybir

F32, BF16 = mybir.dt.float32, mybir.dt.bfloat16
U32 = mybir.dt.uint32
ALU, ACT, AX = mybir.AluOpType, mybir.ActivationFunctionType, mybir.AxisListType

P = 128
EPS = 1e-5
MASKED = -3.0e38
LARGEST_LOG = 80.0

DVE_LINKS = 94
ACT_LINKS = 3


def nth(i, per, k):
    return i * per + (k + 1)


def tower(nc, A, out, scratch):
    B, T = 128, 128
    V, C = A["emb"].shape
    SEQS = 4
    GROUPS = B // SEQS
    N = SEQS * T
    KC, CH = 96, C // 96
    DI = A["out_w"].shape[1]
    MB = DI // P
    L = 3
    NS = A["A_log"].shape[2]
    R = A["dt_w"].shape[1]
    XD = R + 2 * NS
    PAIR = 2
    CPB = NS // PAIR
    CHUNKS = MB * CPB
    BUFS = 4
    E, HD = 3, 64
    H, DH, HG = 12, 16, 4
    HGS = H // HG
    HID = A["ffn_wi"].shape[1]
    FB = HID // P
    STAGES = L + 3
    GATHER = 16 * SEQS

    SIDE = 3
    order = []
    for l in range(L):
        order += [("xT", l, k) for k in range(CH)] + [("in", l, m) for m in range(2 * MB)]
        order += [("x", l)] + [("dt", l, m) for m in range(MB)] + [("out", l, p) for p in range(2)]
    order += [("xT", L, k) for k in range(CH)] + [("gate", 0), ("gate", 1)]
    order += [("qk", m) for m in range(4)] + [("v", p) for p in range(2)]
    order += [("score", 0)]
    for e in range(E):
        order += [("score", e + 1)] * (e + 1 < E) + [("pT", e), ("av", e)]
    order += [("yT", k) for k in range(CH)] + [("proj", p) for p in range(2)]
    order += [("xT", L + 1, k) for k in range(CH)] + [("q", g) for g in range(HGS)]
    order += [("k", g) for g in range(HGS)] + [("v1", p) for p in range(2)]
    order += [("score1", 0)]
    for a in range(H):
        order += [("score1", a + 1)] * (a + 1 < H) + [("pT1", a), ("av1", a)]
    order += [("yT1", k) for k in range(CH)] + [("proj1", p) for p in range(2)]
    order += [("xT", L + 2, k) for k in range(CH)] + [("hid", m) for m in range(FB)]
    order += [("ffn", p) for p in range(2)]
    assert len(set(order)) == len(order)
    place = {name: (j % SIDE, j // SIDE) for j, name in enumerate(order)}
    per_bank = [len(range(b, len(order), SIDE)) for b in range(SIDE)]

    with ExitStack() as ctx:
        def sb(name, shape, dt=F32):
            return ctx.enter_context(nc.sbuf_tensor(name, shape, dt))

        primed = []

        def sem(name, prime=True):
            s = ctx.enter_context(nc.semaphore(name))
            if prime:
                primed.append(s)
            return s

        in_w = sb("in_w", [KC, L, CH, 2 * DI])
        norm_w = sb("norm_w", [KC, 2, CH])
        conv_w = sb("conv_w", [P, L, MB, 4])
        conv_b = sb("conv_b", [P, L, MB])
        x_w = sb("x_w", [P, L, MB, XD])
        dt_w = sb("dt_w", [R, L, DI])
        dt_b = sb("dt_b", [P, L, MB])
        decay = sb("decay", [P, L, MB, NS])
        skip = sb("skip", [P, L, MB])
        out_w = sb("out_w", [P, L, MB, C])
        gate1_w = sb("gate1_w", [KC, CH, 32])
        gate1_b = sb("gate1_b", [32, 1])
        gate2_w = sb("gate2_w", [32, E])
        gate2_b = sb("gate2_b", [1, E])
        qk_w = sb("qk_w", [KC, CH, 2 * C])
        qk_b = sb("qk_b", [P, 4])
        ev_w = sb("ev_w", [KC, CH, C])
        ev_b = sb("ev_b", [1, C])
        ec_w = sb("ec_w", [HD, 3])
        ec_b = sb("ec_b", [HD, 1])
        ep_w = sb("ep_w", [KC, CH, C])
        ep_b = sb("ep_b", [1, C])
        q_w = sb("q_w", [KC, CH, H, 32])
        k_w = sb("k_w", [KC, CH, H, 32])
        q_b = sb("q_b", [P, HGS])
        k_b = sb("k_b", [P, HGS])
        v_w = sb("v_w", [KC, CH, C])
        v_b = sb("v_b", [1, C])
        o_w = sb("o_w", [KC, CH, C])
        o_b = sb("o_b", [1, C])
        ffn_wi = sb("ffn_wi_sb", [KC, CH, HID])
        ffn_bi = sb("ffn_bi_sb", [P, FB])
        ffn_wo = sb("ffn_wo_sb", [P, FB, C])
        ident = sb("ident", [P, P])
        identb = sb("identb", [P, P], BF16)
        causal = sb("causal", [P, SEQS, P], BF16)
        ones = sb("ones", [1, P])
        power = sb("power", [P, SEQS])
        ids = sb("ids", [P, B], mybir.dt.int32)
        idf = sb("idf", [P, B])
        wrap = sb("wrap", [P, B])
        rows = sb("rows", [P, B + SEQS], U32)
        rows_now = sb("rows_now", [P, SEQS], U32)
        embedded = sb("embedded", [P, SEQS, C])
        h = sb("h", [P, SEQS, C])
        result = sb("result", [P, SEQS, C])
        xn = sb("xn", [P, SEQS, C])
        stats = sb("stats", [P, SEQS, 6])
        mean_var = sb("mean_var", [P, SEQS, 2])
        mean_sq = sb("mean_sq", [P, SEQS])
        var = sb("var", [P, SEQS])
        rstd = sb("rstd", [P, SEQS])
        xT = sb("xT", [KC, CH, N])
        arena = sb("arena", [P, 5, MB * N])
        conv, u, gate, delta, w = (arena[:, a, :].rearrange("p (m n) -> p m n", m=MB) for a in range(5))
        soft_e, soft_l, soft_r, y = conv, delta, w, conv
        x_dbl = sb("x_dbl", [XD, N])
        B_all = sb("B_all", [P, NS, N])
        C_all = sb("C_all", [P, NS, N])
        state = [sb(f"state{b}", [P, PAIR, N]) for b in range(BUFS)]
        g1 = sb("g1", [32, N])
        small = sb("small", [P, 16, SEQS, E])
        small1 = sb("small1", [P, 4, SEQS])
        qk = arena[:, 0, :].rearrange("p (m n) -> p m n", m=3)
        q01, k01, q2 = (qk[:, m, :] for m in range(3))
        k2, qc = arena[:, 1, 0:N], arena[:, 1, N:2 * N]
        vv = arena[:, 2, 0:SEQS * C].rearrange("p (b c) -> p b c", b=SEQS)
        mixed = arena[:, 2, SEQS * C:2 * SEQS * C].rearrange("p (b c) -> p b c", b=SEQS)
        probs = [arena[:, 3, x * 512:x * 512 + 512].rearrange("p (h k) -> p h k", k=P) for x in range(2)]
        probsT = [arena[:, 4, x * 512:x * 512 + 512].rearrange("p (h k) -> p h k", k=P) for x in range(2)]
        neg_max = sb("neg_max", [P, 2, SEQS])
        row_max = sb("row_max", [P, 2, SEQS])
        den = sb("den", [P, 2, SEQS])
        rden = sb("rden", [P, 2, SEQS])
        coef = sb("coef", [P, 2, SEQS])
        qT = arena[:, 0, :].rearrange("p (m n) -> p m n", m=HGS)
        kT = arena[:, 1, :].rearrange("p (m n) -> p m n", m=HGS)
        hid = arena[:, 3:5, :].rearrange("p a (m n) -> p (a m) n", n=N)

        dA = [ctx.enter_context(nc.psum_tensor(f"dA{x}", [P, PAIR, N], F32)) for x in range(2)]
        y_sum = ctx.enter_context(nc.psum_tensor("y_sum", [P, N], F32))
        bank = [ctx.enter_context(nc.psum_tensor(f"side{x}", [P, 512], F32)) for x in range(SIDE)]

        loaded = sem("loaded", False)
        ids_loaded = sem("ids_loaded", False)
        gathered = sem("gathered", False)
        stored = sem("stored", False)
        bc_stored = sem("bc_stored", False)
        b_loaded = sem("b_loaded", False)
        c_loaded = sem("c_loaded", False)
        consts = sem("consts", False)
        consts_dve = sem("consts_dve", False)
        log_a_capped = sem("log_a_capped", False)
        log_a = sem("log_a", False)
        set_up = sem("set_up", False)
        rows_ready = sem("rows_ready", False)
        rows_picked = sem("rows_picked", False)
        gate_pool = sem("gate_pool", False)
        gate_dve = sem("gate_dve", False)
        gate_sp = sem("gate_sp", False)
        full = [sem(f"full{x}") for x in range(SIDE)]
        free = [sem(f"free{x}") for x in range(SIDE)]
        var_ready = sem("var_ready")
        rstd_ready = sem("rstd_ready")
        xn_ready = sem("xn_ready")
        u_ready = sem("u_ready")
        soft_ready = sem("soft_ready")
        delta_ready = sem("delta_ready")
        w_ready = sem("w_ready")
        exp_ready = sem("exp_ready")
        input_ready = sem("input_ready")
        scanned = sem("scanned")
        weighed = sem("weighed")
        summed = sem("summed")
        y_free = sem("y_free")
        y_ready = sem("y_ready")
        top_in = sem("top_in")
        top_out = sem("top_out")
        qc_ready = sem("qc_ready")
        max_ready = sem("max_ready")
        dve_link = sem("dve_link")
        act_link = sem("act_link")

        weights = [
            (in_w[:, 0:2], A["in_w"].rearrange("l (k p) n -> p l k n", p=KC)),
            (in_w[:, 2], A["in_w2"].rearrange("(k p) n -> p k n", p=KC)),
            (norm_w[:], A["norm_w"].rearrange("l (k p) -> p l k", p=KC)),
            (conv_w[:, 0:2], A["conv_w"].rearrange("l (m p) o k -> p l m (o k)", p=P)),
            (conv_w[:, 2], A["conv_w2"].rearrange("(m p) o k -> p m (o k)", p=P)),
            (conv_b[:, 0:2], A["conv_b"].rearrange("l (m p) -> p l m", p=P)),
            (conv_b[:, 2], A["conv_b2"].rearrange("(m p) -> p m", p=P)),
            (x_w[:, 0:2], A["x_w"].rearrange("l (m p) n -> p l m n", p=P)),
            (x_w[:, 2], A["x_w2"].rearrange("(m p) n -> p m n", p=P)),
            (dt_w[:, 0:2], A["dt_w"].rearrange("l r n -> r l n")),
            (dt_w[:, 2], A["dt_w2"]),
            (dt_b[:, 0:2], A["dt_b"].rearrange("l (m p) -> p l m", p=P)),
            (dt_b[:, 2], A["dt_b2"].rearrange("(m p) -> p m", p=P)),
            (decay[:, 0:2], A["A_log"].rearrange("l (m p) n -> p l m n", p=P)),
            (decay[:, 2], A["A_log2"].rearrange("(m p) n -> p m n", p=P)),
            (skip[:, 0:2], A["D"].rearrange("l (m p) -> p l m", p=P)),
            (skip[:, 2], A["D2"].rearrange("(m p) -> p m", p=P)),
            (out_w[:, 0:2], A["out_w"].rearrange("l (m p) n -> p l m n", p=P)),
            (out_w[:, 2], A["out_w2"].rearrange("(m p) n -> p m n", p=P)),
            (gate1_w[:], A["Wg1"].rearrange("(k p) n -> p k n", p=KC)),
            (gate1_b[:], A["bg1"].rearrange("(p o) -> p o", o=1)),
            (gate2_w[:], A["Wg2"]),
            (gate2_b[:], A["bg2"].rearrange("(o p) -> o p", o=1)),
            (qk_w[:], A["Wqk"].rearrange("(k p) n -> p k n", p=KC)),
            (qk_b[:, 0:1], A["bqk"][0:P].rearrange("(p o) -> p o", o=1)),
            (qk_b[:, 1:2], A["bqk"][C:C + P].rearrange("(p o) -> p o", o=1)),
            (qk_b[0:HD, 2:3], A["bqk"][P:C].rearrange("(p o) -> p o", o=1)),
            (qk_b[0:HD, 3:4], A["bqk"][C + P:2 * C].rearrange("(p o) -> p o", o=1)),
        ] + [
            (ev_w[:, :, e * HD:(e + 1) * HD], A["Wv"][e].rearrange("(k p) d -> p k d", p=KC)) for e in range(E)
        ] + [
            (ev_b[:], A["bv"].rearrange("(o e) d -> o (e d)", o=1)),
            (ec_w[:], A["ec_w"].rearrange("p o k -> p (o k)")),
            (ec_b[:], A["ec_b"].rearrange("(p o) -> p o", o=1)),
            (ep_w[:], A["Wp"].rearrange("(k p) n -> p k n", p=KC)),
            (ep_b[:], A["bp"].rearrange("(o p) -> o p", o=1)),
            (v_w[:], A["Wv1"].rearrange("(k p) n -> p k n", p=KC)),
            (v_b[:], A["bv1"].rearrange("(o p) -> o p", o=1)),
            (o_w[:], A["Wo"].rearrange("(k p) n -> p k n", p=KC)),
            (o_b[:], A["bo"].rearrange("(o p) -> o p", o=1)),
            (ffn_wi[:], A["ffn_wi"].rearrange("(k p) n -> p k n", p=KC)),
            (ffn_bi[:], A["ffn_bi"].rearrange("(m p) -> p m", p=P)),
            (ffn_wo[:], A["ffn_wo"].rearrange("(m p) n -> p m n", p=P)),
        ]
        padded = []
        for to, name in ((q_w, "Wq"), (k_w, "Wk")):
            for k in range(CH):
                padded.append((to[:, k, :, 0:DH],
                               A[name][k * KC:(k + 1) * KC].rearrange("p (h c) -> p h c", c=DH)))
        for to, name in ((q_b, "bq"), (k_b, "bk")):
            for j in range(HG):
                padded.append((to[32 * j:32 * j + DH, :],
                               A[name].rearrange("(g j c) -> j c g", j=HG, c=DH)[j]))
        LOADED = 16 * (len(weights) + len(padded))

        ctx.enter_context(nc.allow_non_contiguous_dma(reason="small vectors, loaded once"))
        block = ctx.enter_context(nc.Block())

        def hc_buffer(q):
            return state[q % BUFS]

        @block.sync
        def _(sp):
            for s in primed:
                sp.sem_inc(s, 1)
            sp.sem_inc(stored, 16)
            sp.dma_start(ids[:, :], A["ids"]).then_inc(ids_loaded, 16)
            for to, src in weights:
                sp.dma_start(to, src).then_inc(loaded, 16)
            sp.wait_ge(consts_dve, 1)
            for to, src in padded:
                sp.dma_start(to, src).then_inc(loaded, 16)
            with sp.Fori(0, GROUPS) as i:
                for l in range(L):
                    x, k = place[("x", l)]
                    sp.wait_ge(free[x], nth(i, per_bank[x], k + 1))
                    sp.sem_inc(gate_sp, 1)
                    sp.dma_start(scratch[l], x_dbl[R:XD, :]).then_inc(bc_stored, 16)
                    sp.wait_ge(bc_stored, i * (16 * L) + 16 * (l + 1))
                    sp.sem_inc(gate_sp, 1)
                    sp.wait_ge(weighed, nth(i, L * CHUNKS, l * CHUNKS))
                    sp.sem_inc(gate_sp, 1)
                    sp.dma_start(B_all[:, :, :], scratch[l:l + 1, 0:NS, :].broadcast_to([P, NS, N])).then_inc(b_loaded, 16)
                    sp.dma_start(C_all[:, :, :], scratch[l:l + 1, NS:2 * NS, :].broadcast_to([P, NS, N])).then_inc(c_loaded, 16)
                for p in range(2):
                    x, k = place[("ffn", p)]
                    sp.wait_ge(free[x], nth(i, per_bank[x], k + 1))
                    sp.sem_inc(gate_sp, 1)
                sp.dma_start(out.rearrange("(g b) t c -> g t b c", b=SEQS)[i], result[:, :, :]).then_inc(stored, 16)
            sp.wait_ge(stored, 16 * GROUPS + 16)
            sp.wait_ge(bc_stored, 16 * L * GROUPS)

        @block.gpsimd
        def _(pool):
            pool.memset(ident[:, :], 0.0)
            pool.memset(identb[:, :], 0.0)
            pool.memset(causal[:, :, :], 0.0)
            pool.memset(ones[:, :], 1.0)
            pool.memset(power[:, :], -0.5)
            pool.memset(rows[:, B:B + SEQS], 0).then_inc(consts, 1)
            pool.wait_ge(consts, 1)
            pool.affine_select(out=ident[:, :], in_=ident[:, :], compare_op=ALU.not_equal, fill=1.0,
                               base=0, pattern=[[-1, P]], channel_multiplier=1)
            pool.affine_select(out=identb[:, :], in_=identb[:, :], compare_op=ALU.not_equal, fill=1.0,
                               base=0, pattern=[[-1, P]], channel_multiplier=1)
            pool.affine_select(out=causal[:, :, :], in_=causal[:, :, :], compare_op=ALU.is_ge, fill=MASKED,
                               base=0, pattern=[[0, SEQS], [-1, P]], channel_multiplier=1).then_inc(consts, 1)
            pool.wait_ge(rows_ready, 1)
            pool.tensor_copy(rows_now[:, :], rows[:, 0:SEQS]).then_inc(rows_picked, 1)
            pool.wait_ge(rows_picked, 1)
            for b in range(SEQS):
                pool.indirect_dma_start(out=embedded[:, b, :], out_offset=None, in_=A["emb"][:, :],
                                        in_offset=bass.IndirectOffsetOnAxis(ap=rows_now[:, b:b + 1], axis=0)
                                        ).then_inc(gathered, 16)
            with pool.Fori(0, GROUPS) as i:
                def inverse_root(s):
                    pool.wait_ge(var_ready, nth(i, STAGES, s + 1))
                    pool.tensor_tensor(rstd[:, :], var[:, :], power[:, :], ALU.pow).then_inc(rstd_ready, 1)

                for l in range(L):
                    inverse_root(l)
                    if l == 1:
                        pool.wait_ge(gathered, i * GATHER + GATHER)
                        pool.tensor_copy(rows_now[:, :], rows[:, bass.ds((i + 1) * SEQS, SEQS)]).then_inc(rows_picked, 1)
                        pool.wait_ge(rows_picked, i + 2)
                        pool.sem_inc(gate_pool, 1)
                        for b in range(SEQS):
                            pool.indirect_dma_start(
                                out=embedded[:, b, :], out_offset=None, in_=A["emb"][:, :],
                                in_offset=bass.IndirectOffsetOnAxis(ap=rows_now[:, b:b + 1], axis=0)
                            ).then_inc(gathered, 16)
                    pool.wait_ge(delta_ready, nth(i, L, l + 1))
                    pool.wait_ge(u_ready, nth(i, L * MB, (l + 1) * MB))
                    pool.tensor_tensor(w[:, :, :], delta[:, :, :], u[:, :, :], ALU.mult).then_inc(w_ready, 1)
                    pool.wait_ge(w_ready, nth(i, L, l + 1))
                    pool.wait_ge(b_loaded, i * (16 * L) + 16 * (l + 1))
                    for q in range(CHUNKS):
                        d, c = q // CPB, q % CPB
                        Q = l * CHUNKS + q
                        pool.wait_ge(summed, nth(i, L * CHUNKS, Q - BUFS + 1) if Q >= BUFS else nth(i, L * CHUNKS, 0))
                        pool.tensor_tensor(state[Q % BUFS][:, :, :], w[:, d:d + 1, :].broadcast_to([P, PAIR, N]),
                                           B_all[:, PAIR * c:PAIR * c + PAIR, :], ALU.mult).then_inc(input_ready, 1)
                for s in range(L, STAGES):
                    inverse_root(s)
            pool.wait_ge(gathered, GATHER * (GROUPS + 1))

        @block.scalar
        def _(act):
            act.wait_ge(loaded, LOADED)
            act.wait_ge(log_a_capped, 1)
            act.activation(decay[:, :, :, :], decay[:, :, :, :], ACT.Exp).then_inc(log_a, 1)
            act.wait_ge(set_up, 1)
            with act.Fori(0, GROUPS) as i:
                links = [0]

                def link(ins):
                    links[0] += 1
                    ins.then_inc(act_link, 1)
                    act.wait_ge(act_link, nth(i, ACT_LINKS, links[0]))

                def take(name):
                    x, k = place[name]
                    act.wait_ge(full[x], nth(i, per_bank[x], k + 1))
                    return bank[x], free[x]

                for l in range(L):
                    for k in range(CH):
                        tile, freed = take(("xT", l, k))
                        act.activation(xT[:, k, :], tile[0:KC, :], ACT.Copy).then_inc(freed, 1)
                    for m in range(MB):
                        x, k = place[("in", l, m)]
                        act.wait_ge(free[x], nth(i, per_bank[x], k + 1))
                        act.activation(u[:, m, :], conv[:, m, :], ACT.Silu).then_inc(u_ready, 1)
                    for m in range(MB):
                        tile, freed = take(("in", l, MB + m))
                        act.activation(gate[:, m, :], tile[:, :], ACT.Silu).then_inc(freed, 1)
                    tile, freed = take(("x", l))
                    act.activation(x_dbl[:, :], tile[0:XD, :], ACT.Copy).then_inc(freed, 1)
                    for m in range(MB):
                        tile, freed = take(("dt", l, m))
                        bias = dt_b[:, l, m:m + 1]
                        act.activation(soft_r[:, m, :], tile[:, :], ACT.Relu, bias=bias)
                        ins = act.activation(soft_e[:, m, :], tile[:, :], ACT.Abs, bias=bias)
                        ins.then_inc(freed, 1)
                    x, k = place[("dt", l, MB - 1)]
                    act.wait_ge(free[x], nth(i, per_bank[x], k + 1))
                    link(act.activation(soft_e[:, :, :], soft_e[:, :, :], ACT.Exp, scale=-1.0))
                    act.activation(soft_l[:, :, :], soft_e[:, :, :], ACT.Ln, bias=1.0).then_inc(soft_ready, 1)
                    act.wait_ge(delta_ready, nth(i, L, l + 1))
                    for q in range(CHUNKS):
                        d, c = q // CPB, q % CPB
                        Q = l * CHUNKS + q
                        act.wait_ge(scanned, nth(i, L * CHUNKS, max(Q - 1, 0)))
                        for j in range(PAIR):
                            n = PAIR * c + j
                            ins = act.activation(
                                dA[q % 2][:, j, :].rearrange("p (b t) -> p b t", t=T)[:, :, 1:T],
                                delta[:, d, :].rearrange("p (b t) -> p b t", t=T)[:, :, 1:T],
                                ACT.Exp, scale=decay[:, l, d, n:n + 1])
                        ins.then_inc(exp_ready, 1)

                for k in range(CH):
                    tile, freed = take(("xT", L, k))
                    act.activation(xT[:, k, :], tile[0:KC, :], ACT.Copy).then_inc(freed, 1)
                tile, freed = take(("gate", 0))
                act.activation(g1[:, :], tile[0:32, :], ACT.Relu, bias=gate1_b[:, 0:1]).then_inc(freed, 1)
                for m, (to, parts) in enumerate(((q01, P), (k01, P), (q2, HD), (k2, HD))):
                    tile, freed = take(("qk", m))
                    act.activation(to[0:parts, :], tile[0:parts, :], ACT.Identity,
                                   bias=qk_b[0:parts, m:m + 1]).then_inc(freed, 1)
                for p in range(2):
                    tile, freed = take(("v", p))
                    act.activation(vv[:, 2 * p:2 * p + 2, :].rearrange("p b c -> p (b c)"),
                                   tile[:, 0:2 * C], ACT.Copy).then_inc(freed, 1)
                act.wait_ge(top_in, nth(i, 2, 1))
                act.activation(small[:, 1], small[:, 1], ACT.Exp).then_inc(top_out, 1)
                act.wait_ge(top_in, nth(i, 2, 2))
                act.activation(small[:, 3], small[:, 3], ACT.Exp).then_inc(top_out, 1)

                def exps(name, t, scale, before):
                    tile, freed = take(name)
                    act.wait_ge(max_ready, nth(i, E + H, t + 1))
                    if before:
                        x, k = place[before]
                        act.wait_ge(free[x], nth(i, per_bank[x], k + 1))
                    for j in range(SEQS):
                        ins = act.activation(probs[t % 2][:, j, :], tile[:, j * P:(j + 1) * P], ACT.Exp,
                                             bias=neg_max[:, t % 2, j:j + 1], scale=scale,
                                             accum_out=den[:, t % 2, j:j + 1])
                    ins.then_inc(freed, 1)

                def copy_probs(name, t):
                    tile, freed = take(name)
                    act.activation(probsT[t % 2][:, :, :].rearrange("p b k -> p (b k)"), tile[:, :], ACT.Copy).then_inc(freed, 1)

                exps(("score", 0), 0, HD ** -0.5, None)
                for e in range(E):
                    if e + 1 < E:
                        exps(("score", e + 1), e + 1, HD ** -0.5, ("av", e - 1) if e else None)
                    copy_probs(("pT", e), e)
                for k in range(CH):
                    tile, freed = take(("yT", k))
                    act.activation(xT[:, k, :], tile[0:KC, :], ACT.Copy).then_inc(freed, 1)

                for k in range(CH):
                    tile, freed = take(("xT", L + 1, k))
                    act.activation(xT[:, k, :], tile[0:KC, :], ACT.Copy).then_inc(freed, 1)
                for name, to, bias in (("q", qT, q_b), ("k", kT, k_b)):
                    for g in range(HGS):
                        tile, freed = take((name, g))
                        act.activation(to[:, g, :], tile[:, :], ACT.Identity, bias=bias[:, g:g + 1]).then_inc(freed, 1)
                for p in range(2):
                    tile, freed = take(("v1", p))
                    act.activation(vv[:, 2 * p:2 * p + 2, :].rearrange("p b c -> p (b c)"),
                                   tile[:, 0:2 * C], ACT.Copy).then_inc(freed, 1)
                exps(("score1", 0), E, DH ** -0.5, None)
                for a in range(H):
                    if a + 1 < H:
                        exps(("score1", a + 1), E + a + 1, DH ** -0.5, ("av1", a - 1) if a else None)
                    copy_probs(("pT1", a), E + a)
                for k in range(CH):
                    tile, freed = take(("yT1", k))
                    act.activation(xT[:, k, :], tile[0:KC, :], ACT.Copy).then_inc(freed, 1)

                for k in range(CH):
                    tile, freed = take(("xT", L + 2, k))
                    act.activation(xT[:, k, :], tile[0:KC, :], ACT.Copy).then_inc(freed, 1)
                for m in range(FB):
                    tile, freed = take(("hid", m))
                    act.activation(hid[:, m, :], tile[:, :], ACT.Gelu, bias=ffn_bi[:, m:m + 1]).then_inc(freed, 1)
                assert links[0] == ACT_LINKS, f"ACT_LINKS = {links[0]}"


        @block.vector
        def _(dve):
            dve.memset(q_w[:, :, :, :], 0.0)
            dve.memset(k_w[:, :, :, :], 0.0)
            dve.memset(q_b[:, :], 0.0)
            dve.memset(k_b[:, :], 0.0).then_inc(consts_dve, 1)
            for x in range(2):
                dve.memset(dA[x][:, :, :].rearrange("p j (b t) -> p j b t", t=T)[:, :, :, 0:1], 0.0)
            dve.wait_ge(ids_loaded, 16)
            dve.tensor_copy(idf[:, :], ids[:, :]).then_inc(consts_dve, 1)
            dve.wait_ge(consts_dve, 2)
            dve.tensor_scalar(wrap[:, :], idf[:, :], 0.0, float(V), ALU.is_lt, ALU.mult).then_inc(consts_dve, 1)
            dve.wait_ge(consts_dve, 3)
            dve.tensor_tensor(idf[:, :], idf[:, :], wrap[:, :], ALU.add).then_inc(consts_dve, 1)
            dve.wait_ge(consts_dve, 4)
            dve.tensor_scalar(rows[:, 0:B], idf[:, :], 0.0, float(V - 1), ALU.max, ALU.min).then_inc(rows_ready, 1)
            dve.wait_ge(loaded, LOADED)
            dve.tensor_scalar(decay[:, :, :, :], decay[:, :, :, :], LARGEST_LOG, None, ALU.min).then_inc(log_a_capped, 1)
            for l in range(2):
                for k in range(CH):
                    dve.tensor_scalar(in_w[:, l, k, :], in_w[:, l, k, :], norm_w[:, l, k:k + 1], None, ALU.mult)
            dve.wait_ge(log_a, 1)
            dve.tensor_scalar(decay[:, :, :, :], decay[:, :, :, :], -1.0, None, ALU.mult).then_inc(set_up, 1)
            dve.wait_ge(consts, 2)
            with dve.Fori(0, GROUPS) as i:
                links = [0]

                def link(ins):
                    links[0] += 1
                    ins.then_inc(dve_link, 1)
                    dve.wait_ge(dve_link, nth(i, DVE_LINKS, links[0]))

                def take(name):
                    x, k = place[name]
                    dve.wait_ge(full[x], nth(i, per_bank[x], k + 1))
                    return bank[x], free[x]

                def emptied(name):
                    x, k = place[name]
                    dve.wait_ge(free[x], nth(i, per_bank[x], k + 1))

                def norm(s, src):
                    for b in range(SEQS):
                        ins = dve.bn_stats(stats[:, b, :], src[:, b, :])
                    link(ins)
                    dve.sem_inc(gate_dve, 1)
                    for b in range(SEQS):
                        ins = dve.bn_aggr(mean_var[:, b, :], stats[:, b, :])
                    link(ins)
                    if s < 2:
                        link(dve.tensor_tensor(mean_sq[:, :], mean_var[:, :, 0], mean_var[:, :, 0], ALU.mult))
                        dve.scalar_tensor_tensor(out=var[:, :], in0=mean_sq[:, :], scalar=EPS, in1=mean_var[:, :, 1],
                                                 op0=ALU.add, op1=ALU.add).then_inc(var_ready, 1)
                    else:
                        dve.tensor_scalar(var[:, :], mean_var[:, :, 1], EPS, None, ALU.add).then_inc(var_ready, 1)
                    dve.wait_ge(rstd_ready, nth(i, STAGES, s + 1))
                    for b in range(SEQS):
                        if s < 2:
                            ins = dve.tensor_scalar(xn[:, b, :], src[:, b, :], rstd[:, b:b + 1], None, ALU.mult)
                        else:
                            ins = dve.tensor_scalar(xn[:, b, :], src[:, b, :], mean_var[:, b, 0:1], rstd[:, b:b + 1],
                                                    ALU.subtract, ALU.mult)
                    ins.then_inc(xn_ready, 1)

                def residual(stage, to, src, done=None):
                    for p in range(2):
                        tile, freed = take(stage + (p,))
                        dve.tensor_tensor(to[:, 2 * p:2 * p + 2, :], src[:, 2 * p:2 * p + 2, :],
                                          tile[:, 0:2 * C].rearrange("p (b c) -> p b c", b=2), ALU.add).then_inc(freed, 1)
                    for p in range(2):
                        emptied(stage + (p,))

                for l in range(L):
                    src = embedded if l == 0 else h
                    if l == 0:
                        dve.wait_ge(gathered, i * GATHER + GATHER)
                    norm(l, src)
                    for m in range(MB):
                        tile, freed = take(("in", l, m))
                        x = tile[:, :].rearrange("p (b t) -> p b t", t=T)
                        acc = conv[:, m, :].rearrange("p (b t) -> p b t", t=T)
                        link(dve.tensor_scalar(acc, x, conv_w[:, l, m, 3:4], conv_b[:, l, m:m + 1], ALU.mult, ALU.add))
                        for lag in range(1, 4):
                            ins = dve.scalar_tensor_tensor(out=acc[:, :, lag:T], in0=x[:, :, 0:T - lag],
                                                           scalar=conv_w[:, l, m, 3 - lag:4 - lag],
                                                           in1=acc[:, :, lag:T], op0=ALU.mult, op1=ALU.add)
                            if lag < 3:
                                link(ins)
                        ins.then_inc(freed, 1)
                    dve.wait_ge(soft_ready, nth(i, L, l + 1))
                    link(dve.scalar_tensor_tensor(out=soft_e[:, :, :], in0=soft_e[:, :, :], scalar=-2.0, in1=soft_e[:, :, :],
                                                  op0=ALU.add, op1=ALU.mult))
                    link(dve.scalar_tensor_tensor(out=soft_l[:, :, :], in0=soft_e[:, :, :], scalar=-0.5, in1=soft_l[:, :, :],
                                                  op0=ALU.mult, op1=ALU.max))
                    dve.tensor_tensor(delta[:, :, :], soft_l[:, :, :], soft_r[:, :, :], ALU.add).then_inc(delta_ready, 1)
                    dve.wait_ge(c_loaded, i * (16 * L) + 16 * (l + 1))

                    def weigh(Q):
                        c = Q % CPB
                        dve.wait_ge(scanned, nth(i, L * CHUNKS, Q + 1))
                        dve.tensor_tensor(state[Q % BUFS][:, :, :], state[Q % BUFS][:, :, :],
                                          C_all[:, PAIR * c:PAIR * c + PAIR, :], ALU.mult).then_inc(weighed, 1)

                    def finish(d):
                        dve.wait_ge(summed, nth(i, L * CHUNKS, l * CHUNKS + (d + 1) * CPB))
                        dve.scalar_tensor_tensor(out=y[:, d, :], in0=u[:, d, :], scalar=skip[:, l, d:d + 1],
                                                 in1=y_sum[:, :], op0=ALU.mult, op1=ALU.add).then_inc(y_free, 1)
                        dve.wait_ge(y_free, nth(i, L * MB, l * MB + d + 1))
                        dve.tensor_tensor(y[:, d, :], y[:, d, :], gate[:, d, :], ALU.mult).then_inc(y_ready, 1)

                    for q in range(CHUNKS):
                        Q = l * CHUNKS + q
                        dve.wait_ge(exp_ready, nth(i, L * CHUNKS, Q + 1))
                        dve.wait_ge(input_ready, nth(i, L * CHUNKS, Q + 1))
                        flat = state[Q % BUFS][:, :, :].rearrange("p j n -> p (j n)")
                        dve.tensor_tensor_scan(out=flat, data0=dA[q % 2][:, :, :].rearrange("p j n -> p (j n)"), data1=flat,
                                               initial=0.0, op0=ALU.mult, op1=ALU.add).then_inc(scanned, 1)
                        if q:
                            weigh(Q - 1)
                        if q >= CPB and q % CPB == 2:
                            finish(q // CPB - 1)
                    weigh(l * CHUNKS + CHUNKS - 1)
                    finish(MB - 1)
                    residual(("out", l), h, src)

                def maxima(name, t, scale):
                    tile, freed = take(name)
                    link(dve.tensor_reduce(row_max[:, t % 2, :], tile[:, :].rearrange("p (b k) -> p b k", k=P), AX.X, ALU.max))
                    dve.tensor_scalar(neg_max[:, t % 2, :], row_max[:, t % 2, :], -scale, None,
                                      ALU.mult).then_inc(max_ready, 1)

                norm(L, h)
                tile, freed = take(("gate", 1))
                s_ = [small[:, x] for x in range(16)]
                dve.tensor_copy(s_[0], tile[:, 0:SEQS * E].rearrange("p (b e) -> p b e", e=E)).then_inc(freed, 1)
                emptied(("gate", 1))

                def spread(x):
                    return x.unsqueeze(2).broadcast_to([P, SEQS, E])

                link(dve.tensor_reduce(small1[:, 0], s_[0], AX.X, ALU.max))
                dve.tensor_tensor(s_[1], s_[0], spread(small1[:, 0]), ALU.subtract).then_inc(top_in, 1)
                dve.wait_ge(top_out, nth(i, 2, 1))
                link(dve.tensor_reduce(small1[:, 1], s_[1], AX.X, ALU.add))
                link(dve.reciprocal(small1[:, 1], small1[:, 1]))
                link(dve.tensor_tensor(s_[2], s_[1], spread(small1[:, 1]), ALU.mult))
                link(dve.tensor_reduce(small1[:, 2], s_[2], AX.X, ALU.max))
                dve.tensor_tensor(s_[3], s_[2], spread(small1[:, 2]), ALU.subtract).then_inc(top_in, 1)
                p0, p1, p2 = (s_[2][:, :, e] for e in range(E))
                ge, lt, left = s_[4], s_[5], s_[6]
                for x, (a, b) in enumerate(((p0, p1), (p0, p2), (p1, p2))):
                    dve.tensor_tensor(ge[:, :, x], a, b, ALU.is_ge)
                    ins = dve.tensor_tensor(lt[:, :, x], a, b, ALU.is_lt)
                link(ins)
                dve.tensor_tensor(left[:, :, 0], lt[:, :, 0], lt[:, :, 1], ALU.mult)
                dve.tensor_tensor(left[:, :, 1], ge[:, :, 0], lt[:, :, 2], ALU.mult)
                link(dve.tensor_tensor(left[:, :, 2], ge[:, :, 1], ge[:, :, 2], ALU.mult))
                link(dve.tensor_scalar(s_[7], left, -1.0, 1.0, ALU.mult, ALU.add))
                dve.wait_ge(top_out, nth(i, 2, 2))
                link(dve.tensor_tensor(s_[8], s_[3], s_[7], ALU.mult))
                link(dve.tensor_reduce(small1[:, 3], s_[8], AX.X, ALU.add))
                link(dve.reciprocal(small1[:, 3], small1[:, 3]))
                link(dve.tensor_tensor(s_[9], s_[8], spread(small1[:, 3]), ALU.mult))
                emptied(("qk", 0))
                x = q01[0:HD, :].rearrange("p (b t) -> p b t", t=T)
                acc = qc[0:HD, :].rearrange("p (b t) -> p b t", t=T)
                link(dve.tensor_scalar(acc, x, ec_w[:, 1:2], ec_b[:, 0:1], ALU.mult, ALU.add))
                link(dve.scalar_tensor_tensor(out=acc[:, :, 1:T], in0=x[:, :, 0:T - 1], scalar=ec_w[:, 0:1],
                                              in1=acc[:, :, 1:T], op0=ALU.mult, op1=ALU.add))
                dve.scalar_tensor_tensor(out=acc[:, :, 0:T - 1], in0=x[:, :, 1:T], scalar=ec_w[:, 2:3],
                                         in1=acc[:, :, 0:T - 1], op0=ALU.mult, op1=ALU.add).then_inc(qc_ready, 1)
                maxima(("score", 0), 0, HD ** -0.5)
                for e in range(E):
                    if e + 1 < E:
                        maxima(("score", e + 1), e + 1, HD ** -0.5)
                    tile, freed = take(("av", e))
                    link(dve.reciprocal(rden[:, e % 2, :], den[:, e % 2, :]))
                    link(dve.tensor_tensor(coef[:, e % 2, :], rden[:, e % 2, :], s_[9][:, :, e], ALU.mult))
                    dve.tensor_tensor(mixed[:, :, e * HD:(e + 1) * HD], tile[:, 0:SEQS * HD].rearrange("p (b d) -> p b d", b=SEQS),
                                      coef[:, e % 2, :].unsqueeze(2).broadcast_to([P, SEQS, HD]), ALU.mult).then_inc(freed, 1)
                residual(("proj",), h, h)

                norm(L + 1, h)
                maxima(("score1", 0), E, DH ** -0.5)
                for a in range(H):
                    t = E + a
                    if a + 1 < H:
                        maxima(("score1", a + 1), t + 1, DH ** -0.5)
                    tile, freed = take(("av1", a))
                    link(dve.reciprocal(rden[:, t % 2, :], den[:, t % 2, :]))
                    dve.tensor_tensor(mixed[:, :, a * DH:(a + 1) * DH], tile[:, 0:SEQS * DH].rearrange("p (b d) -> p b d", b=SEQS),
                                      rden[:, t % 2, :].unsqueeze(2).broadcast_to([P, SEQS, DH]), ALU.mult).then_inc(freed, 1)
                residual(("proj1",), h, h)

                norm(L + 2, h)
                dve.wait_ge(stored, i * 16 + 16)
                for p in range(2):
                    tile, freed = take(("ffn", p))
                    dve.tensor_tensor(result[:, 2 * p:2 * p + 2, :], h[:, 2 * p:2 * p + 2, :],
                                      tile[:, 0:2 * C].rearrange("p (b c) -> p b c", b=2), ALU.add).then_inc(freed, 1)
                assert links[0] == DVE_LINKS, f"DVE_LINKS = {links[0]}"

        @block.tensor
        def _(pe):
            pe.wait_ge(set_up, 1)
            pe.wait_ge(consts, 2)
            with pe.Fori(0, GROUPS) as i:
                def fill(name):
                    x, k = place[name]
                    pe.wait_ge(free[x], nth(i, per_bank[x], k))
                    return bank[x], full[x]

                def emptied(name):
                    x, k = place[name]
                    pe.wait_ge(free[x], nth(i, per_bank[x], k + 1))

                def turn(name, src):
                    for k in range(CH):
                        tile, filled = fill(name + (k,))
                        for b in range(SEQS):
                            ins = pe.transpose(tile[0:KC, b * T:(b + 1) * T], src[:, b, k * KC:(k + 1) * KC], ident[:, :])
                        ins.then_inc(filled, 1)

                def project(name, weight, bias=None):
                    for p in range(2):
                        tile, filled = fill(name + (p,))
                        for b in range(2 * p, 2 * p + 2):
                            to = tile[:, (b % 2) * C:(b % 2 + 1) * C]
                            for k in range(CH):
                                ins = pe.matmul(to, xT[:, k, b * T:(b + 1) * T], weight[:, k, :], start=k == 0, stop=False)
                            ins = pe.matmul(to, ones[:, :], bias[:, :], start=False, stop=True)
                        ins.then_inc(filled, 1)

                for l in range(L):
                    pe.wait_ge(xn_ready, nth(i, STAGES, l + 1))
                    turn(("xT", l), xn)
                    for k in range(CH):
                        emptied(("xT", l, k))
                    for m in range(2 * MB):
                        tile, filled = fill(("in", l, m))
                        for k in range(CH):
                            ins = pe.matmul(tile[:, :], in_w[:, l, k, m * P:(m + 1) * P], xT[:, k, :],
                                            start=k == 0, stop=k == CH - 1)
                        ins.then_inc(filled, 1)
                    tile, filled = fill(("x", l))
                    for m in range(MB):
                        pe.wait_ge(u_ready, nth(i, L * MB, l * MB + m + 1))
                        ins = pe.matmul(tile[0:XD, :], x_w[:, l, m, :], u[:, m, :], start=m == 0, stop=m == MB - 1)
                    ins.then_inc(filled, 1)
                    emptied(("x", l))
                    for m in range(MB):
                        tile, filled = fill(("dt", l, m))
                        pe.matmul(tile[:, :], dt_w[:, l, m * P:(m + 1) * P], x_dbl[0:R, :],
                                  start=True, stop=True).then_inc(filled, 1)
                    for q in range(CHUNKS):
                        d, c = q // CPB, q % CPB
                        Q = l * CHUNKS + q
                        if c == 0:
                            pe.wait_ge(y_free, nth(i, L * MB, l * MB + d))
                        pe.wait_ge(weighed, nth(i, L * CHUNKS, Q + 1))
                        for j in range(PAIR):
                            ins = pe.matmul(y_sum[:, :], ident[:, :], state[Q % BUFS][:, j, :],
                                            start=c == 0 and j == 0, stop=c == CPB - 1 and j == PAIR - 1)
                        ins.then_inc(summed, 1)
                    for p in range(2):
                        tile, filled = fill(("out", l, p))
                        if p == 0:
                            pe.wait_ge(y_ready, nth(i, L * MB, (l + 1) * MB))
                        for b in range(2 * p, 2 * p + 2):
                            for m in range(MB):
                                ins = pe.matmul(tile[:, (b % 2) * C:(b % 2 + 1) * C], y[:, m, b * T:(b + 1) * T],
                                                out_w[:, l, m, :], start=m == 0, stop=m == MB - 1)
                        ins.then_inc(filled, 1)

                def values(name, weight, bias):
                    for p in range(2):
                        tile, filled = fill((name, p))
                        for b in range(2 * p, 2 * p + 2):
                            to = tile[:, (b % 2) * C:(b % 2 + 1) * C]
                            for k in range(CH):
                                pe.matmul(to, xT[:, k, b * T:(b + 1) * T], weight[:, k, :], start=k == 0, stop=False)
                            ins = pe.matmul(to, ones[:, :], bias[:, :], start=False, stop=True)
                        ins.then_inc(filled, 1)

                def turn_probs(name, score, t):
                    emptied(score)
                    tile, filled = fill(name)
                    for j in range(SEQS):
                        ins = pe.transpose(tile[:, j * P:(j + 1) * P], probs[t % 2][:, j, :], ident[:, :])
                    ins.then_inc(filled, 1)

                pe.wait_ge(xn_ready, nth(i, STAGES, L + 1))
                turn(("xT", L), xn)
                for k in range(CH):
                    emptied(("xT", L, k))
                tile, filled = fill(("gate", 0))
                for k in range(CH):
                    ins = pe.matmul(tile[0:32, :], gate1_w[:, k, :], xT[:, k, :], start=k == 0, stop=k == CH - 1)
                ins.then_inc(filled, 1)
                emptied(("gate", 0))
                tile, filled = fill(("gate", 1))
                for b in range(SEQS):
                    to = tile[:, b * E:(b + 1) * E]
                    pe.matmul(to, g1[:, b * T:(b + 1) * T], gate2_w[:, :], start=True, stop=False)
                    ins = pe.matmul(to, ones[:, :], gate2_b[:, :], start=False, stop=True)
                ins.then_inc(filled, 1)
                for m, (first, parts) in enumerate(((0, P), (C, P), (P, HD), (C + P, HD))):
                    tile, filled = fill(("qk", m))
                    for k in range(CH):
                        ins = pe.matmul(tile[0:parts, :], qk_w[:, k, first:first + parts], xT[:, k, :],
                                        start=k == 0, stop=k == CH - 1)
                    ins.then_inc(filled, 1)
                values("v", ev_w, ev_b)

                def expert_scores(e):
                    tile, filled = fill(("score", e))
                    pe.matmul(tile[:, :], identb[:, :], causal[:, :, :].rearrange("p b k -> p (b k)"),
                              start=True, stop=False, skip_group_check=True)
                    q_, k_ = ((qc[0:HD], k01[0:HD]), (q01[HD:P], k01[HD:P]), (q2[0:HD], k2[0:HD]))[e]
                    for b in range(SEQS):
                        at = slice(b * T, (b + 1) * T)
                        ins = pe.matmul(tile[:, at], q_[:, at], k_[:, at], start=False, stop=True, skip_group_check=True)
                    ins.then_inc(filled, 1)

                pe.wait_ge(qc_ready, nth(i, 1, 1))
                emptied(("qk", 3))
                for p in range(2):
                    emptied(("v", p))
                expert_scores(0)
                for e in range(E):
                    if e + 1 < E:
                        expert_scores(e + 1)
                    turn_probs(("pT", e), ("score", e), e)
                    emptied(("pT", e))
                    tile, filled = fill(("av", e))
                    for b in range(SEQS):
                        ins = pe.matmul(tile[:, b * HD:(b + 1) * HD], probsT[e % 2][:, b, :],
                                        vv[:, b, e * HD:(e + 1) * HD], start=True, stop=True)
                    ins.then_inc(filled, 1)
                emptied(("av", E - 1))
                turn(("yT",), mixed)
                for k in range(CH):
                    emptied(("yT", k))
                project(("proj",), ep_w, ep_b)

                pe.wait_ge(xn_ready, nth(i, STAGES, L + 2))
                turn(("xT", L + 1), xn)
                for k in range(CH):
                    emptied(("xT", L + 1, k))
                for name, weight in (("q", q_w), ("k", k_w)):
                    for g in range(HGS):
                        tile, filled = fill((name, g))
                        for k in range(CH):
                            ins = pe.matmul(tile[:, :], weight[:, k, g * HG:(g + 1) * HG, :].rearrange("p h c -> p (h c)"),
                                            xT[:, k, :], start=k == 0, stop=k == CH - 1)
                        ins.then_inc(filled, 1)
                values("v1", v_w, v_b)

                def head_scores(a):
                    rows_, g = slice(32 * (a % HG), 32 * (a % HG) + 32), a // HG
                    tile, filled = fill(("score1", a))
                    for b in range(SEQS):
                        at = slice(b * T, (b + 1) * T)
                        ins = pe.matmul(tile[:, at], qT[rows_, g, at], kT[rows_, g, at], start=True, stop=True)
                    ins.then_inc(filled, 1)

                emptied(("k", HGS - 1))
                for p in range(2):
                    emptied(("v1", p))
                head_scores(0)
                for a in range(H):
                    t = E + a
                    if a + 1 < H:
                        head_scores(a + 1)
                    turn_probs(("pT1", a), ("score1", a), t)
                    emptied(("pT1", a))
                    tile, filled = fill(("av1", a))
                    for b in range(SEQS):
                        ins = pe.matmul(tile[:, b * DH:(b + 1) * DH], probsT[t % 2][:, b, :],
                                        vv[:, b, a * DH:(a + 1) * DH], start=True, stop=True)
                    ins.then_inc(filled, 1)
                emptied(("av1", H - 1))
                turn(("yT1",), mixed)
                for k in range(CH):
                    emptied(("yT1", k))
                project(("proj1",), o_w, o_b)

                pe.wait_ge(xn_ready, nth(i, STAGES, L + 3))
                turn(("xT", L + 2), xn)
                for k in range(CH):
                    emptied(("xT", L + 2, k))
                for m in range(FB):
                    tile, filled = fill(("hid", m))
                    for k in range(CH):
                        ins = pe.matmul(tile[:, :], ffn_wi[:, k, m * P:(m + 1) * P], xT[:, k, :],
                                        start=k == 0, stop=k == CH - 1)
                    ins.then_inc(filled, 1)
                for m in range(FB - SIDE, FB):
                    emptied(("hid", m))
                for p in range(2):
                    tile, filled = fill(("ffn", p))
                    for b in range(2 * p, 2 * p + 2):
                        for m in range(FB):
                            ins = pe.matmul(tile[:, (b % 2) * C:(b % 2 + 1) * C], hid[:, m, b * T:(b + 1) * T],
                                            ffn_wo[:, m, :], start=m == 0, stop=m == FB - 1)
                    ins.then_inc(filled, 1)


_INS = {
    "ids": "x", "emb": "L0_tok_emb", "norm_w": "L0_tok_norm_w", "in_w": "L0_tok_in_proj_w",
    "conv_w": "L0_tok_conv_w", "conv_b": "L0_tok_conv_b", "x_w": "L0_tok_x_proj_w", "dt_w": "L0_tok_dt_proj_w",
    "dt_b": "L0_tok_dt_proj_b", "A_log": "L0_tok_A_log", "D": "L0_tok_D", "out_w": "L0_tok_out_proj_w",
    "in_w2": "L0_attn_W_in", "conv_w2": "L0_attn_conv_w", "conv_b2": "L0_attn_conv_b", "x_w2": "L0_attn_W_x",
    "dt_w2": "L0_attn_W_dt", "dt_b2": "L0_attn_b_dt", "A_log2": "L0_attn_A_log", "D2": "L0_attn_D",
    "out_w2": "L0_attn_W_out", "Wqk": "L0_ffn_Wqk", "bqk": "L0_ffn_bqk", "Wv": "L0_ffn_Wv", "bv": "L0_ffn_bv",
    "ec_w": "L0_ffn_conv_w", "ec_b": "L0_ffn_conv_b", "Wg1": "L0_ffn_Wg1", "bg1": "L0_ffn_bg1",
    "Wg2": "L0_ffn_Wg2", "bg2": "L0_ffn_bg2", "Wp": "L0_ffn_Wp", "bp": "L0_ffn_bp",
    "Wq": "L1_attn_Wq", "bq": "L1_attn_bq", "Wk": "L1_attn_Wk", "bk": "L1_attn_bk", "Wv1": "L1_attn_Wv",
    "bv1": "L1_attn_bv", "Wo": "L1_attn_Wo", "bo": "L1_attn_bo", "ffn_wi": "L1_ffn_in_weight",
    "ffn_bi": "L1_ffn_in_bias", "ffn_wo": "L1_ffn_out_weight",
}
_TRANSPOSED = ("ids", "ffn_wi")


def kernel(**inputs):
    import numpy as _np
    import concourse.bacc as _bacc
    from concourse import mybir as _mybir
    from concourse.bass_utils import run_bass_kernel_spmd as _run

    nc = _bacc.Bacc("TRN2", target_bir_lowering=False, num_devices=1)
    arrays, A = {}, {}
    for name, given in _INS.items():
        a = _np.asarray(inputs[given])
        a = _np.ascontiguousarray(a.T if name in _TRANSPOSED else a)
        arrays[f"in_{name}_dram"] = a
        A[name] = nc.dram_tensor(f"in_{name}_dram", a.shape, _mybir.dt.from_np(a.dtype), kind="ExternalInput").ap()
    out = nc.dram_tensor("out_0_dram", (128, 128, 192), _mybir.dt.float32, kind="ExternalOutput").ap()
    scratch = nc.dram_tensor("bc_dram", (3, 32, 512), _mybir.dt.float32, kind="Internal").ap()
    tower(nc, A, out, scratch)
    r = _run(nc, [arrays], core_ids=[0])
    return r.results[0]["out_0_dram"]
```

```python
from contextlib import ExitStack

import concourse.bass as bass
from concourse import mybir

F32, BF16 = mybir.dt.float32, mybir.dt.bfloat16
U32 = mybir.dt.uint32
ALU, ACT, AX = mybir.AluOpType, mybir.ActivationFunctionType, mybir.AxisListType

P = 128
EPS = 1e-5
MASKED = -3.0e38
LARGEST_LOG = 80.0
EXP_SET = "natural_log_exp_and_others"

DVE_LINKS = 188
ACT_LINKS = 6


def nth(i, per, k):
    return i * per + (k + 1)


def side_by_side(*tasks):
    tasks = list(tasks)
    while tasks:
        tasks = [task for task in tasks if next(task, "ended") != "ended"]


def tower(nc, A, out, scratch):
    B, T = 128, 128
    V, C = A["emb"].shape
    SEQS = 4
    S = 2
    ROUNDS = B // (SEQS * S)
    N = SEQS * T
    KC, CH = 96, C // 96
    DI = A["out_w"].shape[1]
    MB = DI // P
    L = 3
    NS = A["A_log"].shape[2]
    R = A["dt_w"].shape[1]
    XD = R + 2 * NS
    SCANS = S * L
    BUFS = 4
    ROWS_B = 4
    DECAYS = 3
    SIDE = 2
    E, HD = 3, 64
    H, DH, HG = 12, 16, 4
    HGS = H // HG
    HID = A["ffn_wi"].shape[1]
    FB = HID // P
    STAGES = L + 3
    GATHER = 16 * SEQS
    TILES = S * (STAGES * CH + L * (2 * MB + 1 + MB + 2) + (2 + 4 + 2 + 3 * E + CH + 2)
                 + (2 * HGS + 2 + 3 * H + CH + 2) + (FB + 2))
    place = {}
    per_bank = [len(range(x, TILES, SIDE)) for x in range(SIDE)]
    with ExitStack() as ctx:
        def sb(name, shape, dt=F32):
            return ctx.enter_context(nc.sbuf_tensor(name, shape, dt))

        primed = []

        def sem(name, prime=True):
            s = ctx.enter_context(nc.semaphore(name))
            if prime:
                primed.append(s)
            return s

        in_w = sb("in_w", [KC, L, CH, 2 * DI])
        norm_w = sb("norm_w", [KC, 2, CH])
        conv_w = sb("conv_w", [P, L, MB, 4])
        conv_b = sb("conv_b", [P, L, MB])
        x_w = sb("x_w", [P, L, MB, XD])
        dt_w = sb("dt_w", [R, L, DI])
        dt_b = sb("dt_b", [P, L, MB])
        decay = sb("decay", [P, L, MB, NS])
        skip = sb("skip", [P, L, MB])
        out_w = sb("out_w", [P, L, MB, C])
        gate1_w = sb("gate1_w", [KC, CH, 32])
        gate1_b = sb("gate1_b", [32, 1])
        gate2_w = sb("gate2_w", [32, E])
        gate2_b = sb("gate2_b", [1, E])
        qk_w = sb("qk_w", [KC, CH, 2 * C])
        qk_b = sb("qk_b", [P, 4])
        ev_w = sb("ev_w", [KC, CH, C])
        ev_b = sb("ev_b", [1, C])
        ec_w = sb("ec_w", [HD, 3])
        ec_b = sb("ec_b", [HD, 1])
        ep_w = sb("ep_w", [KC, CH, C])
        ep_b = sb("ep_b", [1, C])
        q_w = sb("q_w", [KC, CH, H, 32])
        k_w = sb("k_w", [KC, CH, H, 32])
        q_b = sb("q_b", [P, HGS])
        k_b = sb("k_b", [P, HGS])
        v_w = sb("v_w", [KC, CH, C])
        v_b = sb("v_b", [1, C])
        o_w = sb("o_w", [KC, CH, C])
        o_b = sb("o_b", [1, C])
        ffn_wi = sb("ffn_wi_sb", [KC, CH, HID])
        ffn_bi = sb("ffn_bi_sb", [P, FB])
        ffn_wo = sb("ffn_wo_sb", [P, FB, C])
        ident = sb("ident", [P, P])
        identb = sb("identb", [P, P], BF16)
        causal = sb("causal", [P, SEQS, P], BF16)
        ones = sb("ones", [1, P])
        power = sb("power", [P, SEQS])
        rows = sb("rows", [P, B + SEQS * S], U32)
        rows_now = sb("rows_now", [P, S, SEQS], U32)
        h = [sb(f"h{s}", [P, SEQS, C]) for s in range(S)]
        result = sb("result", [P, SEQS, C])
        xn = [sb(f"xn{s}", [P, SEQS, C]) for s in range(S)]
        stats = sb("stats", [P, S, SEQS, 6])
        mean_var = sb("mean_var", [P, S, SEQS, 2])
        mean_sq = sb("mean_sq", [P, S, SEQS])
        var = sb("var", [P, S, SEQS])
        rstd = sb("rstd", [P, S, SEQS])
        xT = [sb(f"xT{s}", [KC, CH, N]) for s in range(S)]
        arena = [sb(f"arena{s}", [P, 5, MB * N]) for s in range(S)]

        def part(a, s, m):
            return arena[s][:, a, :].rearrange("p (m n) -> p m n", m=m)

        conv, u, gate, delta, w = ([part(a, s, MB) for s in range(S)] for a in range(5))
        soft_e, soft_l, soft_r, y = conv, delta, w, conv
        x_dbl = [sb(f"x_dbl{s}", [XD, N]) for s in range(S)]
        bc = [sb(f"bc{x}", [P, 2, N]) for x in range(ROWS_B)]
        state = [sb(f"state{x}", [P, MB, N]) for x in range(BUFS)]
        ids = state[0][:, 0, 0:B].bitcast(mybir.dt.int32)
        idf, wrap = state[0][:, 1, 0:B], state[0][:, 2, 0:B]
        g1 = [sb(f"g1_{s}", [32, N]) for s in range(S)]
        small = sb("small", [P, S, 16, SEQS, E])
        small1 = sb("small1", [P, S, 4, SEQS])
        q01, k01, q2 = ([part(0, s, 3)[:, m, :] for s in range(S)] for m in range(3))
        k2, qc = ([part(1, s, 3)[:, m, :] for s in range(S)] for m in range(2))
        vv, mixed = ([arena[s][:, 2, x * SEQS * C:(x + 1) * SEQS * C].rearrange("p (b c) -> p b c", b=SEQS)
                      for s in range(S)] for x in range(2))
        probs, probsT = ([[part(a, s, 3)[:, x, :].rearrange("p (b k) -> p b k", k=P) for x in range(2)]
                          for s in range(S)] for a in (3, 4))
        neg_max, row_max, den, rden, coef = (sb(name, [P, S, 2, SEQS])
                                             for name in ("neg_max", "row_max", "den", "rden", "coef"))
        qT, kT = ([part(a, s, HGS) for s in range(S)] for a in range(2))
        hid = [arena[s][:, 3:5, :].rearrange("p a (m n) -> p (a m) n", n=N) for s in range(S)]

        dA = [ctx.enter_context(nc.psum_tensor(f"dA{x}", [P, N], F32)) for x in range(DECAYS)]
        y_sum = [ctx.enter_context(nc.psum_tensor(f"y_sum{d}", [P, N], F32)) for d in range(MB)]
        bank = [ctx.enter_context(nc.psum_tensor(f"side{x}", [P, 512], F32)) for x in range(SIDE)]

        loaded = sem("loaded", False)
        ids_loaded = sem("ids_loaded", False)
        gathered = [sem(f"gathered{s}", False) for s in range(S)]
        stored = sem("stored", False)
        bc_stored = [sem(f"bc_stored{s}", False) for s in range(S)]
        bc_loaded = [sem(f"bc_loaded{x}", False) for x in range(ROWS_B)]
        consts = sem("consts", False)
        consts_dve = sem("consts_dve", False)
        log_a_capped = sem("log_a_capped", False)
        log_a = sem("log_a", False)
        set_up = sem("set_up", False)
        rows_ready = sem("rows_ready", False)
        rows_picked = sem("rows_picked", False)
        gate_pool = sem("gate_pool", False)
        gate_dve = sem("gate_dve", False)
        gate_sp = sem("gate_sp", False)
        full = [sem(f"full{x}") for x in range(SIDE)]
        free = [sem(f"free{x}") for x in range(SIDE)]

        def each(name):
            return [sem(f"{name}{s}") for s in range(S)]

        var_ready, rstd_ready, xn_ready = each("var_ready"), each("rstd_ready"), each("xn_ready")
        u_ready, gate_in, gate_ready = each("u_ready"), each("gate_in"), each("gate_ready")
        abs_ready, soft_ready, delta_ready, w_ready = each("abs_ready"), each("soft_ready"), each("delta_ready"), each("w_ready")
        y_ready = each("y_ready")
        top_in, top_out, qc_ready, max_ready = each("top_in"), each("top_out"), each("qc_ready"), each("max_ready")
        hid_ready = each("hid_ready")
        exp_ready = sem("exp_ready")
        input_ready = sem("input_ready")
        scanned = sem("scanned")
        weighed = sem("weighed")
        summed = sem("summed")
        y_free = sem("y_free")
        dve_link = sem("dve_link")
        act_link = sem("act_link")

        weights = [
            (in_w[:, 0:2], A["in_w"].rearrange("l (k p) n -> p l k n", p=KC)),
            (in_w[:, 2], A["in_w2"].rearrange("(k p) n -> p k n", p=KC)),
            (norm_w[:], A["norm_w"].rearrange("l (k p) -> p l k", p=KC)),
            (conv_w[:, 0:2], A["conv_w"].rearrange("l (m p) o k -> p l m (o k)", p=P)),
            (conv_w[:, 2], A["conv_w2"].rearrange("(m p) o k -> p m (o k)", p=P)),
            (conv_b[:, 0:2], A["conv_b"].rearrange("l (m p) -> p l m", p=P)),
            (conv_b[:, 2], A["conv_b2"].rearrange("(m p) -> p m", p=P)),
            (x_w[:, 0:2], A["x_w"].rearrange("l (m p) n -> p l m n", p=P)),
            (x_w[:, 2], A["x_w2"].rearrange("(m p) n -> p m n", p=P)),
            (dt_w[:, 0:2], A["dt_w"].rearrange("l r n -> r l n")),
            (dt_w[:, 2], A["dt_w2"]),
            (dt_b[:, 0:2], A["dt_b"].rearrange("l (m p) -> p l m", p=P)),
            (dt_b[:, 2], A["dt_b2"].rearrange("(m p) -> p m", p=P)),
            (decay[:, 0:2], A["A_log"].rearrange("l (m p) n -> p l m n", p=P)),
            (decay[:, 2], A["A_log2"].rearrange("(m p) n -> p m n", p=P)),
            (skip[:, 0:2], A["D"].rearrange("l (m p) -> p l m", p=P)),
            (skip[:, 2], A["D2"].rearrange("(m p) -> p m", p=P)),
            (out_w[:, 0:2], A["out_w"].rearrange("l (m p) n -> p l m n", p=P)),
            (out_w[:, 2], A["out_w2"].rearrange("(m p) n -> p m n", p=P)),
            (gate1_w[:], A["Wg1"].rearrange("(k p) n -> p k n", p=KC)),
            (gate1_b[:], A["bg1"].rearrange("(p o) -> p o", o=1)),
            (gate2_w[:], A["Wg2"]),
            (gate2_b[:], A["bg2"].rearrange("(o p) -> o p", o=1)),
            (qk_w[:], A["Wqk"].rearrange("(k p) n -> p k n", p=KC)),
            (qk_b[:, 0:1], A["bqk"][0:P].rearrange("(p o) -> p o", o=1)),
            (qk_b[:, 1:2], A["bqk"][C:C + P].rearrange("(p o) -> p o", o=1)),
            (qk_b[0:HD, 2:3], A["bqk"][P:C].rearrange("(p o) -> p o", o=1)),
            (qk_b[0:HD, 3:4], A["bqk"][C + P:2 * C].rearrange("(p o) -> p o", o=1)),
        ] + [
            (ev_w[:, :, e * HD:(e + 1) * HD], A["Wv"][e].rearrange("(k p) d -> p k d", p=KC)) for e in range(E)
        ] + [
            (ev_b[:], A["bv"].rearrange("(o e) d -> o (e d)", o=1)),
            (ec_w[:], A["ec_w"].rearrange("p o k -> p (o k)")),
            (ec_b[:], A["ec_b"].rearrange("(p o) -> p o", o=1)),
            (ep_w[:], A["Wp"].rearrange("(k p) n -> p k n", p=KC)),
            (ep_b[:], A["bp"].rearrange("(o p) -> o p", o=1)),
            (v_w[:], A["Wv1"].rearrange("(k p) n -> p k n", p=KC)),
            (v_b[:], A["bv1"].rearrange("(o p) -> o p", o=1)),
            (o_w[:], A["Wo"].rearrange("(k p) n -> p k n", p=KC)),
            (o_b[:], A["bo"].rearrange("(o p) -> o p", o=1)),
            (ffn_wi[:], A["ffn_wi"].rearrange("(k p) n -> p k n", p=KC)),
            (ffn_bi[:], A["ffn_bi"].rearrange("(m p) -> p m", p=P)),
            (ffn_wo[:], A["ffn_wo"].rearrange("(m p) n -> p m n", p=P)),
        ]
        padded = []
        for to, name in ((q_w, "Wq"), (k_w, "Wk")):
            for k in range(CH):
                padded.append((to[:, k, :, 0:DH],
                               A[name][k * KC:(k + 1) * KC].rearrange("p (h c) -> p h c", c=DH)))
        for to, name in ((q_b, "bq"), (k_b, "bk")):
            for j in range(HG):
                padded.append((to[32 * j:32 * j + DH, :],
                               A[name].rearrange("(g j c) -> j c g", j=HG, c=DH)[j]))
        LOADED = 16 * (len(weights) + len(padded))

        ctx.enter_context(nc.allow_non_contiguous_dma(reason="small vectors, loaded once"))
        block = ctx.enter_context(nc.Block())

        def chunk(s, l, n):
            return (l * S + s) * NS + n

        def phases(scan, post, norm, before, experts, heads, mlp, scan_last=False):
            def beside(*tasks):
                side_by_side(*(reversed(tasks) if scan_last else tasks))

            def onward(s, l):
                if l:
                    yield from post(s, l - 1)
                yield from norm(s, l)
                yield
                yield from (before(s, l) if l < L else experts(s))

            side_by_side(onward(0, 0))
            for l in range(L):
                beside(scan(0, l), onward(1, l))
                beside(scan(1, l), onward(0, l + 1))
            side_by_side(heads(0), onward(1, L))
            side_by_side(heads(1), mlp(0))
            side_by_side(mlp(1))

        @block.tensor
        def _(pe):
            pe.wait_ge(set_up, 1)
            pe.wait_ge(consts, 2)
            with pe.Fori(0, ROUNDS) as i:
                waited = [0] * SIDE

                def wait_free(x, tiles):
                    if tiles > waited[x] or not tiles:
                        pe.wait_ge(free[x], nth(i, per_bank[x], tiles))
                    waited[x] = max(tiles, waited[x])

                def fill(name):
                    x, k = place[name] = len(place) % SIDE, len(place) // SIDE
                    wait_free(x, k)
                    return bank[x], full[x]

                def emptied(name):
                    x, k = place[name]
                    wait_free(x, k + 1)

                def turn(name, src):
                    for k in range(CH):
                        tile, filled = fill(name + (k,))
                        for b in range(SEQS):
                            ins = pe.transpose(tile[0:KC, b * T:(b + 1) * T], src[:, b, k * KC:(k + 1) * KC], ident[:, :])
                        ins.then_inc(filled, 1)

                def from_xT(name, s, weight, m):
                    tile, filled = fill(name)
                    for k in range(CH):
                        ins = pe.matmul(tile[0:m, :], weight(k), xT[s][:, k, :], start=k == 0, stop=k == CH - 1)
                    ins.then_inc(filled, 1)

                def to_tokens(name, s, weight, bias):
                    for p in range(2):
                        tile, filled = fill(name + (p,))
                        for b in range(2 * p, 2 * p + 2):
                            to = tile[:, (b % 2) * C:(b % 2 + 1) * C]
                            for k in range(CH):
                                pe.matmul(to, xT[s][:, k, b * T:(b + 1) * T], weight[:, k, :], start=k == 0, stop=False)
                            ins = pe.matmul(to, ones[:, :], bias[:, :], start=False, stop=True)
                        ins.then_inc(filled, 1)

                def scan(s, l):
                    yield
                    yield
                    for n in range(NS):
                        Q = chunk(s, l, n)
                        pe.wait_ge(weighed, nth(i, SCANS * NS, Q + 1))
                        for d in range(MB):
                            if n == 0:
                                pe.wait_ge(y_free, nth(i, SCANS * MB, (l * S + s - 1) * MB + d + 1 if l or s else 0))
                            ins = pe.matmul(y_sum[d][:, :], ident[:, :], state[Q % BUFS][:, d, :],
                                            start=n == 0, stop=n == NS - 1)
                        ins.then_inc(summed, 1)
                        yield

                def post(s, l):
                    yield
                    pe.wait_ge(y_ready[s], nth(i, L, l + 1))
                    for p in range(2):
                        tile, filled = fill(("out", s, l, p))
                        for b in range(2 * p, 2 * p + 2):
                            for m in range(MB):
                                ins = pe.matmul(tile[:, (b % 2) * C:(b % 2 + 1) * C], y[s][:, m, b * T:(b + 1) * T],
                                                out_w[:, l, m, :], start=m == 0, stop=m == MB - 1)
                        ins.then_inc(filled, 1)
                    yield

                def norm(s, stage):
                    yield
                    yield
                    pe.wait_ge(xn_ready[s], nth(i, STAGES, stage + 1))
                    turn(("xT", s, stage), xn[s])

                def turned(s, stage):
                    for k in range(CH):
                        emptied(("xT", s, stage, k))

                def before(s, l):
                    turned(s, l)

                    def inner(m):
                        from_xT(("in", s, l, m), s, lambda k: in_w[:, l, k, m * P:(m + 1) * P], P)

                    inner(0)
                    inner(1)
                    yield
                    for m in range(2, 2 * MB):
                        inner(m)
                        yield
                    tile, filled = fill(("x", s, l))
                    pe.wait_ge(u_ready[s], nth(i, L, l + 1))
                    for m in range(MB):
                        ins = pe.matmul(tile[0:XD, :], x_w[:, l, m, :], u[s][:, m, :], start=m == 0, stop=m == MB - 1)
                    ins.then_inc(filled, 1)
                    yield
                    emptied(("x", s, l))
                    for m in range(MB):
                        tile, filled = fill(("dt", s, l, m))
                        pe.matmul(tile[:, :], dt_w[:, l, m * P:(m + 1) * P], x_dbl[s][0:R, :],
                                  start=True, stop=True).then_inc(filled, 1)
                        if m == 1:
                            yield
                    yield
                    yield
                    yield

                def turn_probs(name, score, s, t):
                    emptied(score)
                    tile, filled = fill(name)
                    for b in range(SEQS):
                        ins = pe.transpose(tile[:, b * P:(b + 1) * P], probs[s][t % 2][:, b, :], ident[:, :])
                    ins.then_inc(filled, 1)

                def weighted_values(name, turned_probs, s, t, first, width):
                    emptied(turned_probs)
                    tile, filled = fill(name)
                    for b in range(SEQS):
                        ins = pe.matmul(tile[:, b * width:(b + 1) * width], probsT[s][t % 2][:, b, :],
                                        vv[s][:, b, first:first + width], start=True, stop=True)
                    ins.then_inc(filled, 1)

                def experts(s):
                    turned(s, L)
                    from_xT(("gate", s, 0), s, lambda k: gate1_w[:, k, :], 32)
                    yield
                    emptied(("gate", s, 0))
                    tile, filled = fill(("gate", s, 1))
                    for b in range(SEQS):
                        to = tile[:, b * E:(b + 1) * E]
                        pe.matmul(to, g1[s][:, b * T:(b + 1) * T], gate2_w[:, :], start=True, stop=False)
                        ins = pe.matmul(to, ones[:, :], gate2_b[:, :], start=False, stop=True)
                    ins.then_inc(filled, 1)
                    yield
                    for m, (first, parts) in enumerate(((0, P), (C, P), (P, HD), (C + P, HD))):
                        from_xT(("qk", s, m), s, lambda k: qk_w[:, k, first:first + parts], parts)
                        if m % 2:
                            yield
                    to_tokens(("v", s), s, ev_w, ev_b)
                    yield

                    def expert_scores(e):
                        tile, filled = fill(("score", s, e))
                        pe.matmul(tile[:, :], identb[:, :], causal[:, :, :].rearrange("p b k -> p (b k)"),
                                  start=True, stop=False, skip_group_check=True)
                        q_, k_ = ((qc[s][0:HD], k01[s][0:HD]), (q01[s][HD:P], k01[s][HD:P]), (q2[s][0:HD], k2[s][0:HD]))[e]
                        for b in range(SEQS):
                            at = slice(b * T, (b + 1) * T)
                            ins = pe.matmul(tile[:, at], q_[:, at], k_[:, at], start=False, stop=True, skip_group_check=True)
                        ins.then_inc(filled, 1)

                    pe.wait_ge(qc_ready[s], nth(i, 1, 1))
                    for p in range(2):
                        emptied(("v", s, p))
                    expert_scores(0)
                    yield
                    for e in range(E):
                        if e + 1 < E:
                            expert_scores(e + 1)
                        turn_probs(("pT", s, e), ("score", s, e), s, e)
                        yield
                        weighted_values(("av", s, e), ("pT", s, e), s, e, e * HD, HD)
                        yield
                    emptied(("av", s, E - 1))
                    turn(("yT", s), mixed[s])
                    yield
                    for k in range(CH):
                        emptied(("yT", s, k))
                    to_tokens(("proj", s), s, ep_w, ep_b)

                def heads(s):
                    yield from norm(s, L + 1)
                    yield
                    turned(s, L + 1)
                    for x in range(2 * HGS):
                        g, weight = x % HGS, (q_w, k_w)[x // HGS]
                        from_xT(("q", s, x), s, lambda k: weight[:, k, g * HG:(g + 1) * HG, :].rearrange("p h c -> p (h c)"), P)
                        if x % 2:
                            yield
                    to_tokens(("v1", s), s, v_w, v_b)
                    yield

                    def head_scores(a):
                        rows_, g = slice(32 * (a % HG), 32 * (a % HG) + 32), a // HG
                        tile, filled = fill(("score1", s, a))
                        for b in range(SEQS):
                            at = slice(b * T, (b + 1) * T)
                            ins = pe.matmul(tile[:, at], qT[s][rows_, g, at], kT[s][rows_, g, at], start=True, stop=True)
                        ins.then_inc(filled, 1)

                    for p in range(2):
                        emptied(("v1", s, p))
                    head_scores(0)
                    yield
                    for a in range(H):
                        if a + 1 < H:
                            head_scores(a + 1)
                        turn_probs(("pT1", s, a), ("score1", s, a), s, E + a)
                        yield
                        weighted_values(("av1", s, a), ("pT1", s, a), s, E + a, a * DH, DH)
                        yield
                    emptied(("av1", s, H - 1))
                    turn(("yT1", s), mixed[s])
                    yield
                    for k in range(CH):
                        emptied(("yT1", s, k))
                    to_tokens(("proj1", s), s, o_w, o_b)

                def mlp(s):
                    yield from norm(s, L + 2)
                    yield
                    turned(s, L + 2)
                    for m in range(FB):
                        from_xT(("hid", s, m), s, lambda k: ffn_wi[:, k, m * P:(m + 1) * P], P)
                        if m % 2:
                            yield
                    pe.wait_ge(hid_ready[s], nth(i, 1, 1))
                    for p in range(2):
                        tile, filled = fill(("ffn", s, p))
                        for b in range(2 * p, 2 * p + 2):
                            for m in range(FB):
                                ins = pe.matmul(tile[:, (b % 2) * C:(b % 2 + 1) * C], hid[s][:, m, b * T:(b + 1) * T],
                                                ffn_wo[:, m, :], start=m == 0, stop=m == FB - 1)
                        ins.then_inc(filled, 1)
                    yield

                phases(scan, post, norm, before, experts, heads, mlp, scan_last=True)
                assert len(place) == TILES, f"TILES = {len(place)}"

        @block.sync
        def _(sp):
            for x in primed:
                sp.sem_inc(x, 1)
            sp.sem_inc(stored, 16)
            sp.dma_start(ids, A["ids"]).then_inc(ids_loaded, 16)
            for to, src in weights:
                sp.dma_start(to, src).then_inc(loaded, 16)
            sp.wait_ge(consts_dve, 1)
            for to, src in padded:
                sp.dma_start(to, src).then_inc(loaded, 16)
            with sp.Fori(0, ROUNDS) as i:
                def scan(s, l):
                    for n in range(NS):
                        Q = chunk(s, l, n)
                        if n == 0:
                            sp.wait_ge(bc_stored[s], i * (16 * L) + 16 * (l + 1))
                            sp.sem_inc(gate_sp, 1)
                        sp.wait_ge(weighed, nth(i, SCANS * NS, max(Q - ROWS_B + 1, 0)))
                        sp.sem_inc(gate_sp, 1)
                        sp.dma_start(bc[Q % ROWS_B][:, :, :], scratch[s:s + 1, :, n, :].broadcast_to([P, 2, N])
                                     ).then_inc(bc_loaded[Q % ROWS_B], 16)
                        yield

                def post(s, l):
                    yield
                    yield

                def norm(s, stage):
                    yield
                    yield

                def before(s, l):
                    for slot in range(7):
                        yield
                    x, k = place[("x", s, l)]
                    sp.wait_ge(free[x], nth(i, per_bank[x], k + 1))
                    sp.sem_inc(gate_sp, 1)
                    sp.dma_start(scratch[s].rearrange("a n t -> (a n) t"), x_dbl[s][R:XD, :]).then_inc(bc_stored[s], 16)
                    for slot in range(3):
                        yield

                def experts(s):
                    yield

                def heads(s):
                    yield

                def mlp(s):
                    for slot in range(6):
                        yield
                    for p in range(2):
                        x, k = place[("ffn", s, p)]
                        sp.wait_ge(free[x], nth(i, per_bank[x], k + 1))
                        sp.sem_inc(gate_sp, 1)
                    sp.dma_start(out.rearrange("(g b) t c -> g t b c", b=SEQS)[i * S + s], result[:, :, :]).then_inc(stored, 16)

                phases(scan, post, norm, before, experts, heads, mlp)
            sp.wait_ge(stored, 16 * S * ROUNDS + 16)
            for s in range(S):
                sp.wait_ge(bc_stored[s], 16 * L * ROUNDS)

        @block.gpsimd
        def _(pool):
            pool.memset(ident[:, :], 0.0)
            pool.memset(identb[:, :], 0.0)
            pool.memset(causal[:, :, :], 0.0)
            pool.memset(ones[:, :], 1.0)
            pool.memset(power[:, :], -0.5)
            pool.memset(rows[:, B:B + SEQS * S], 0).then_inc(consts, 1)
            pool.wait_ge(consts, 1)
            pool.affine_select(out=ident[:, :], in_=ident[:, :], compare_op=ALU.not_equal, fill=1.0,
                               base=0, pattern=[[-1, P]], channel_multiplier=1)
            pool.affine_select(out=identb[:, :], in_=identb[:, :], compare_op=ALU.not_equal, fill=1.0,
                               base=0, pattern=[[-1, P]], channel_multiplier=1)
            pool.affine_select(out=causal[:, :, :], in_=causal[:, :, :], compare_op=ALU.is_ge, fill=MASKED,
                               base=0, pattern=[[0, SEQS], [-1, P]], channel_multiplier=1).then_inc(consts, 1)

            def gather(s):
                for b in range(SEQS):
                    pool.indirect_dma_start(out=h[s][:, b, :], out_offset=None, in_=A["emb"][:, :],
                                            in_offset=bass.IndirectOffsetOnAxis(ap=rows_now[:, s, b:b + 1], axis=0)
                                            ).then_inc(gathered[s], 16)

            pool.wait_ge(rows_ready, 1)
            pool.tensor_copy(rows_now[:, :, :], rows[:, 0:S * SEQS].rearrange("p (s b) -> p s b", s=S)).then_inc(rows_picked, 1)
            pool.wait_ge(rows_picked, 1)
            for s in range(S):
                gather(s)
            with pool.Fori(0, ROUNDS) as i:
                def scan(s, l):
                    for n in range(NS):
                        Q = chunk(s, l, n)
                        if n == 0:
                            pool.wait_ge(w_ready[s], nth(i, L, l + 1))
                        pool.wait_ge(bc_loaded[Q % ROWS_B], i * (16 * SCANS * NS // ROWS_B) + 16 * (Q // ROWS_B + 1))
                        pool.wait_ge(summed, nth(i, SCANS * NS, max(Q - BUFS + 1, 0)))
                        pool.tensor_tensor(state[Q % BUFS][:, :, :], w[s][:, :, :],
                                           bc[Q % ROWS_B][:, 0:1, :].broadcast_to([P, MB, N]), ALU.mult).then_inc(input_ready, 1)
                        yield

                def post(s, l):
                    yield
                    yield

                def norm(s, stage):
                    pool.wait_ge(var_ready[s], nth(i, STAGES, stage + 1))
                    pool.tensor_tensor(rstd[:, s, :], var[:, s, :], power[:, :], ALU.pow).then_inc(rstd_ready[s], 1)
                    yield
                    yield

                def before(s, l):
                    for slot in range(10):
                        yield
                    pool.wait_ge(delta_ready[s], nth(i, L, l + 1))
                    pool.tensor_tensor(w[s][:, :, :], delta[s][:, :, :], u[s][:, :, :], ALU.mult).then_inc(w_ready[s], 1)

                def experts(s):
                    yield

                def heads(s):
                    yield from norm(s, L + 1)

                def mlp(s):
                    yield from norm(s, L + 2)
                    for slot in range(4):
                        yield
                    for p in range(2):
                        x, k = place[("ffn", s, p)]
                        pool.wait_ge(free[x], nth(i, per_bank[x], k + 1))
                    pool.tensor_copy(rows_now[:, s, :], rows[:, bass.ds((i + 1) * (SEQS * S) + s * SEQS, SEQS)]
                                     ).then_inc(rows_picked, 1)
                    pool.wait_ge(rows_picked, i * S + (s + 2))
                    pool.sem_inc(gate_pool, 1)
                    gather(s)

                phases(scan, post, norm, before, experts, heads, mlp)
            for s in range(S):
                pool.wait_ge(gathered[s], GATHER * (ROUNDS + 1))

        @block.scalar
        def _(act):
            act.wait_ge(loaded, LOADED)
            act.wait_ge(log_a_capped, 1)
            act.activation(decay[:, :, :, :], decay[:, :, :, :], ACT.Exp).then_inc(log_a, 1)
            act.wait_ge(set_up, 1)
            act.preload_act_table_set(EXP_SET)
            with act.Fori(0, ROUNDS) as i:
                links = [0]

                def link(ins):
                    links[0] += 1
                    ins.then_inc(act_link, 1)
                    act.wait_ge(act_link, nth(i, ACT_LINKS, links[0]))

                def take(name):
                    x, k = place[name]
                    act.wait_ge(full[x], nth(i, per_bank[x], k + 1))
                    return bank[x], free[x]

                def emptied(name):
                    x, k = place[name]
                    act.wait_ge(free[x], nth(i, per_bank[x], k + 1))

                def copy(name, to, parts=P, func=ACT.Copy, **how):
                    tile, freed = take(name)
                    act.activation(to, tile[0:parts, :], func, **how).then_inc(freed, 1)

                def copy_values(name, s):
                    for p in range(2):
                        tile, freed = take(name + (p,))
                        act.activation(vv[s][:, 2 * p:2 * p + 2, :].rearrange("p b c -> p (b c)"),
                                       tile[:, 0:2 * C], ACT.Copy).then_inc(freed, 1)

                def scan(s, l):
                    for n in range(NS):
                        if n == 0:
                            act.wait_ge(delta_ready[s], nth(i, L, l + 1))
                        for d in range(MB):
                            X = chunk(s, l, n) * MB + d
                            act.wait_ge(scanned, nth(i, SCANS * NS * MB, max(X - DECAYS + 1, 0)))
                            act.activation(dA[X % DECAYS][:, :].rearrange("p (b t) -> p b t", t=T)[:, :, 1:T],
                                           delta[s][:, d, :].rearrange("p (b t) -> p b t", t=T)[:, :, 1:T],
                                           ACT.Exp, scale=decay[:, l, d, n:n + 1]).then_inc(exp_ready, 1)
                        yield

                def post(s, l):
                    yield
                    yield

                def norm(s, stage):
                    yield
                    yield
                    for k in range(CH):
                        copy(("xT", s, stage, k), xT[s][:, k, :], KC)

                def before(s, l):
                    yield
                    yield
                    for m in range(MB):
                        copy(("in", s, l, MB + m), gate[s][:, m, :])
                        if m < MB - 1:
                            yield
                    for m in range(MB - 2, MB):
                        emptied(("in", s, l, m))
                    act.activation(u[s][:, :, :], conv[s][:, :, :], ACT.Silu).then_inc(u_ready[s], 1)
                    for m in range(2 * MB - 2, 2 * MB):
                        emptied(("in", s, l, m))
                    act.activation(gate[s][:, :, :], gate[s][:, :, :], ACT.Silu).then_inc(gate_ready[s], 1)
                    act.preload_act_table_set(EXP_SET)
                    yield
                    copy(("x", s, l), x_dbl[s][:, :], XD)
                    yield
                    for m in range(MB):
                        tile, freed = take(("dt", s, l, m))
                        bias = dt_b[:, l, m:m + 1]
                        act.activation(soft_r[s][:, m, :], tile[:, :], ACT.Relu, bias=bias)
                        act.activation(soft_e[s][:, m, :], tile[:, :], ACT.Abs, bias=bias).then_inc(freed, 1)
                        if m == 1:
                            yield
                    yield
                    for m in range(1, MB):
                        emptied(("dt", s, l, m))
                    link(act.activation(soft_e[s][:, :, :], soft_e[s][:, :, :], ACT.Exp, scale=-1.0))
                    act.activation(soft_l[s][:, :, :], soft_e[s][:, :, :], ACT.Ln, bias=1.0).then_inc(soft_ready[s], 1)
                    yield
                    yield

                def exps(name, s, t, scale, before_):
                    tile, freed = take(name)
                    act.wait_ge(max_ready[s], nth(i, E + H, t + 1))
                    if before_:
                        emptied(before_)
                    for b in range(SEQS):
                        ins = act.activation(probs[s][t % 2][:, b, :], tile[:, b * P:(b + 1) * P], ACT.Exp,
                                             bias=neg_max[:, s, t % 2, b:b + 1], scale=scale,
                                             accum_out=den[:, s, t % 2, b:b + 1])
                    ins.then_inc(freed, 1)

                def copy_probs(name, s, t):
                    copy(name, probsT[s][t % 2][:, :, :].rearrange("p b k -> p (b k)"))

                def experts(s):
                    copy(("gate", s, 0), g1[s][:, :], 32, ACT.Relu, bias=gate1_b[:, 0:1])
                    yield
                    act.wait_ge(top_in[s], nth(i, 2, 1))
                    act.activation(small[:, s, 1], small[:, s, 1], ACT.Exp).then_inc(top_out[s], 1)
                    yield
                    for m, (to, parts) in enumerate(((q01, P), (k01, P), (q2, HD), (k2, HD))):
                        copy(("qk", s, m), to[s][0:parts, :], parts, ACT.Identity, bias=qk_b[0:parts, m:m + 1])
                        if m == 1:
                            act.wait_ge(top_in[s], nth(i, 2, 2))
                            act.activation(small[:, s, 3], small[:, s, 3], ACT.Exp).then_inc(top_out[s], 1)
                        if m % 2:
                            yield
                    copy_values(("v", s), s)
                    yield
                    exps(("score", s, 0), s, 0, HD ** -0.5, None)
                    yield
                    for e in range(E):
                        if e + 1 < E:
                            exps(("score", s, e + 1), s, e + 1, HD ** -0.5, ("av", s, e - 1) if e else None)
                        copy_probs(("pT", s, e), s, e)
                        yield
                        yield
                    for k in range(CH):
                        copy(("yT", s, k), xT[s][:, k, :], KC)
                    yield

                def heads(s):
                    yield from norm(s, L + 1)
                    yield
                    for x in range(2 * HGS):
                        g = x % HGS
                        to, bias = ((qT, q_b), (kT, k_b))[x // HGS]
                        copy(("q", s, x), to[s][:, g, :], P, ACT.Identity, bias=bias[:, g:g + 1])
                        if x % 2:
                            yield
                    copy_values(("v1", s), s)
                    yield
                    exps(("score1", s, 0), s, E, DH ** -0.5, None)
                    yield
                    for a in range(H):
                        if a + 1 < H:
                            exps(("score1", s, a + 1), s, E + a + 1, DH ** -0.5, ("av1", s, a - 1) if a else None)
                        copy_probs(("pT1", s, a), s, E + a)
                        yield
                        yield
                    for k in range(CH):
                        copy(("yT1", s, k), xT[s][:, k, :], KC)
                    yield

                def mlp(s):
                    yield from norm(s, L + 2)
                    yield
                    for m in range(FB):
                        copy(("hid", s, m), hid[s][:, m, :], P, ACT.Identity, bias=ffn_bi[:, m:m + 1])
                        if m == FB - 1:
                            for x in range(FB - 2, FB):
                                emptied(("hid", s, x))
                            act.activation(hid[s][:, :, :], hid[s][:, :, :], ACT.Gelu).then_inc(hid_ready[s], 1)
                            act.preload_act_table_set(EXP_SET)
                        if m % 2:
                            yield
                    yield

                phases(scan, post, norm, before, experts, heads, mlp)
                assert links[0] == ACT_LINKS, f"ACT_LINKS = {links[0]}"

        @block.vector
        def _(dve):
            dve.memset(q_w[:, :, :, :], 0.0)
            dve.memset(k_w[:, :, :, :], 0.0)
            dve.memset(q_b[:, :], 0.0)
            dve.memset(k_b[:, :], 0.0).then_inc(consts_dve, 1)
            for x in range(DECAYS):
                dve.memset(dA[x][:, :].rearrange("p (b t) -> p b t", t=T)[:, :, 0:1], 0.0)
            dve.wait_ge(ids_loaded, 16)
            dve.tensor_copy(idf, ids).then_inc(consts_dve, 1)
            dve.wait_ge(consts_dve, 2)
            dve.tensor_scalar(wrap, idf, 0.0, float(V), ALU.is_lt, ALU.mult).then_inc(consts_dve, 1)
            dve.wait_ge(consts_dve, 3)
            dve.tensor_tensor(idf, idf, wrap, ALU.add).then_inc(consts_dve, 1)
            dve.wait_ge(consts_dve, 4)
            dve.tensor_scalar(rows[:, 0:B], idf, 0.0, float(V - 1), ALU.max, ALU.min).then_inc(rows_ready, 1)
            dve.wait_ge(loaded, LOADED)
            dve.tensor_scalar(decay[:, :, :, :], decay[:, :, :, :], LARGEST_LOG, None, ALU.min).then_inc(log_a_capped, 1)
            for l in range(2):
                for k in range(CH):
                    dve.tensor_scalar(in_w[:, l, k, :], in_w[:, l, k, :], norm_w[:, l, k:k + 1], None, ALU.mult)
            dve.wait_ge(log_a, 1)
            dve.tensor_scalar(decay[:, :, :, :], decay[:, :, :, :], -1.0, None, ALU.mult).then_inc(set_up, 1)
            dve.wait_ge(consts, 2)
            with dve.Fori(0, ROUNDS) as i:
                links = [0]

                def link(ins):
                    links[0] += 1
                    ins.then_inc(dve_link, 1)
                    dve.wait_ge(dve_link, nth(i, DVE_LINKS, links[0]))

                def take(name):
                    x, k = place[name]
                    dve.wait_ge(full[x], nth(i, per_bank[x], k + 1))
                    return bank[x], free[x]

                def emptied(name):
                    x, k = place[name]
                    dve.wait_ge(free[x], nth(i, per_bank[x], k + 1))

                def residual(name, s):
                    for p in range(2):
                        tile, freed = take(name + (p,))
                        dve.tensor_tensor(h[s][:, 2 * p:2 * p + 2, :], h[s][:, 2 * p:2 * p + 2, :],
                                          tile[:, 0:2 * C].rearrange("p (b c) -> p b c", b=2), ALU.add).then_inc(freed, 1)

                def scan(s, l):
                    def weigh(Q):
                        dve.wait_ge(scanned, nth(i, SCANS * NS * MB, (Q + 1) * MB))
                        dve.tensor_tensor(state[Q % BUFS][:, :, :], state[Q % BUFS][:, :, :],
                                          bc[Q % ROWS_B][:, 1:2, :].broadcast_to([P, MB, N]), ALU.mult).then_inc(weighed, 1)

                    for n in range(NS):
                        Q = chunk(s, l, n)
                        dve.wait_ge(bc_loaded[Q % ROWS_B], i * (16 * SCANS * NS // ROWS_B) + 16 * (Q // ROWS_B + 1))
                        dve.wait_ge(input_ready, nth(i, SCANS * NS, Q + 1))
                        for d in range(MB):
                            X = Q * MB + d
                            dve.wait_ge(exp_ready, nth(i, SCANS * NS * MB, X + 1))
                            dve.tensor_tensor_scan(out=state[Q % BUFS][:, d, :], data0=dA[X % DECAYS][:, :],
                                                   data1=state[Q % BUFS][:, d, :], initial=0.0,
                                                   op0=ALU.mult, op1=ALU.add).then_inc(scanned, 1)
                        if n:
                            weigh(Q - 1)
                        yield
                    weigh(chunk(s, l, NS - 1))

                def post(s, l):
                    dve.wait_ge(summed, nth(i, SCANS * NS, chunk(s, l, NS)))
                    dve.wait_ge(gate_ready[s], nth(i, L, l + 1))
                    for d in range(MB):
                        dve.scalar_tensor_tensor(out=y[s][:, d, :], in0=u[s][:, d, :], scalar=skip[:, l, d:d + 1],
                                                 in1=y_sum[d][:, :], op0=ALU.mult, op1=ALU.add).then_inc(y_free, 1)
                    dve.wait_ge(y_free, nth(i, SCANS * MB, (l * S + s + 1) * MB))
                    dve.tensor_tensor(y[s][:, :, :], y[s][:, :, :], gate[s][:, :, :], ALU.mult).then_inc(y_ready[s], 1)
                    yield
                    yield
                    residual(("out", s, l), s)
                    for p in range(2):
                        emptied(("out", s, l, p))

                def norm(s, stage):
                    if stage == 0:
                        dve.wait_ge(gathered[s], i * GATHER + GATHER)
                    for b in range(SEQS):
                        ins = dve.bn_stats(stats[:, s, b, :], h[s][:, b, :])
                    link(ins)
                    dve.sem_inc(gate_dve, 1)
                    for b in range(SEQS):
                        ins = dve.bn_aggr(mean_var[:, s, b, :], stats[:, s, b, :])
                    link(ins)
                    if stage < 2:
                        link(dve.tensor_tensor(mean_sq[:, s, :], mean_var[:, s, :, 0], mean_var[:, s, :, 0], ALU.mult))
                        dve.scalar_tensor_tensor(out=var[:, s, :], in0=mean_sq[:, s, :], scalar=EPS, in1=mean_var[:, s, :, 1],
                                                 op0=ALU.add, op1=ALU.add).then_inc(var_ready[s], 1)
                    else:
                        dve.tensor_scalar(var[:, s, :], mean_var[:, s, :, 1], EPS, None, ALU.add).then_inc(var_ready[s], 1)
                    yield
                    dve.wait_ge(rstd_ready[s], nth(i, STAGES, stage + 1))
                    for b in range(SEQS):
                        if stage < 2:
                            ins = dve.tensor_scalar(xn[s][:, b, :], h[s][:, b, :], rstd[:, s, b:b + 1], None, ALU.mult)
                        else:
                            ins = dve.tensor_scalar(xn[s][:, b, :], h[s][:, b, :], mean_var[:, s, b, 0:1], rstd[:, s, b:b + 1],
                                                    ALU.subtract, ALU.mult)
                    ins.then_inc(xn_ready[s], 1)
                    yield

                def before(s, l):
                    for m in range(MB):
                        tile, freed = take(("in", s, l, m))
                        x = tile[:, :].rearrange("p (b t) -> p b t", t=T)
                        acc = conv[s][:, m, :].rearrange("p (b t) -> p b t", t=T)
                        link(dve.tensor_scalar(acc, x, conv_w[:, l, m, 3:4], conv_b[:, l, m:m + 1], ALU.mult, ALU.add))
                        for lag in range(1, 4):
                            ins = dve.scalar_tensor_tensor(out=acc[:, :, lag:T], in0=x[:, :, 0:T - lag],
                                                           scalar=conv_w[:, l, m, 3 - lag:4 - lag],
                                                           in1=acc[:, :, lag:T], op0=ALU.mult, op1=ALU.add)
                            if lag < 3:
                                link(ins)
                        ins.then_inc(freed, 1)
                        yield
                    for slot in range(6):
                        yield
                    dve.wait_ge(soft_ready[s], nth(i, L, l + 1))
                    link(dve.scalar_tensor_tensor(out=soft_e[s][:, :, :], in0=soft_e[s][:, :, :], scalar=-2.0,
                                                  in1=soft_e[s][:, :, :], op0=ALU.add, op1=ALU.mult))
                    link(dve.scalar_tensor_tensor(out=soft_l[s][:, :, :], in0=soft_e[s][:, :, :], scalar=-0.5,
                                                  in1=soft_l[s][:, :, :], op0=ALU.mult, op1=ALU.max))
                    dve.tensor_tensor(delta[s][:, :, :], soft_l[s][:, :, :], soft_r[s][:, :, :], ALU.add).then_inc(delta_ready[s], 1)
                    yield

                def maxima(name, s, t, scale):
                    tile, freed = take(name)
                    link(dve.tensor_reduce(row_max[:, s, t % 2, :], tile[:, :].rearrange("p (b k) -> p b k", k=P), AX.X, ALU.max))
                    dve.tensor_scalar(neg_max[:, s, t % 2, :], row_max[:, s, t % 2, :], -scale, None,
                                      ALU.mult).then_inc(max_ready[s], 1)

                def experts(s):
                    s_ = [small[:, s, x] for x in range(16)]
                    s1 = [small1[:, s, x] for x in range(4)]

                    def spread(x):
                        return x.unsqueeze(2).broadcast_to([P, SEQS, E])

                    yield
                    tile, freed = take(("gate", s, 1))
                    dve.tensor_copy(s_[0], tile[:, 0:SEQS * E].rearrange("p (b e) -> p b e", e=E)).then_inc(freed, 1)
                    emptied(("gate", s, 1))
                    link(dve.tensor_reduce(s1[0], s_[0], AX.X, ALU.max))
                    dve.tensor_tensor(s_[1], s_[0], spread(s1[0]), ALU.subtract).then_inc(top_in[s], 1)
                    yield
                    dve.wait_ge(top_out[s], nth(i, 2, 1))
                    link(dve.tensor_reduce(s1[1], s_[1], AX.X, ALU.add))
                    link(dve.reciprocal(s1[1], s1[1]))
                    link(dve.tensor_tensor(s_[2], s_[1], spread(s1[1]), ALU.mult))
                    link(dve.tensor_reduce(s1[2], s_[2], AX.X, ALU.max))
                    dve.tensor_tensor(s_[3], s_[2], spread(s1[2]), ALU.subtract).then_inc(top_in[s], 1)
                    yield
                    p0, p1, p2 = (s_[2][:, :, e] for e in range(E))
                    ge, lt, left = s_[4], s_[5], s_[6]
                    for x, (a, b) in enumerate(((p0, p1), (p0, p2), (p1, p2))):
                        dve.tensor_tensor(ge[:, :, x], a, b, ALU.is_ge)
                        ins = dve.tensor_tensor(lt[:, :, x], a, b, ALU.is_lt)
                    link(ins)
                    dve.tensor_tensor(left[:, :, 0], lt[:, :, 0], lt[:, :, 1], ALU.mult)
                    dve.tensor_tensor(left[:, :, 1], ge[:, :, 0], lt[:, :, 2], ALU.mult)
                    link(dve.tensor_tensor(left[:, :, 2], ge[:, :, 1], ge[:, :, 2], ALU.mult))
                    link(dve.tensor_scalar(s_[7], left, -1.0, 1.0, ALU.mult, ALU.add))
                    dve.wait_ge(top_out[s], nth(i, 2, 2))
                    link(dve.tensor_tensor(s_[8], s_[3], s_[7], ALU.mult))
                    link(dve.tensor_reduce(s1[3], s_[8], AX.X, ALU.add))
                    link(dve.reciprocal(s1[3], s1[3]))
                    link(dve.tensor_tensor(s_[9], s_[8], spread(s1[3]), ALU.mult))
                    yield
                    emptied(("qk", s, 0))
                    x = q01[s][0:HD, :].rearrange("p (b t) -> p b t", t=T)
                    acc = qc[s][0:HD, :].rearrange("p (b t) -> p b t", t=T)
                    link(dve.tensor_scalar(acc, x, ec_w[:, 1:2], ec_b[:, 0:1], ALU.mult, ALU.add))
                    link(dve.scalar_tensor_tensor(out=acc[:, :, 1:T], in0=x[:, :, 0:T - 1], scalar=ec_w[:, 0:1],
                                                  in1=acc[:, :, 1:T], op0=ALU.mult, op1=ALU.add))
                    dve.scalar_tensor_tensor(out=acc[:, :, 0:T - 1], in0=x[:, :, 1:T], scalar=ec_w[:, 2:3],
                                             in1=acc[:, :, 0:T - 1], op0=ALU.mult, op1=ALU.add).then_inc(qc_ready[s], 1)
                    yield
                    maxima(("score", s, 0), s, 0, HD ** -0.5)
                    yield
                    for e in range(E):
                        if e + 1 < E:
                            maxima(("score", s, e + 1), s, e + 1, HD ** -0.5)
                        yield
                        tile, freed = take(("av", s, e))
                        at = (slice(None), s, e % 2)
                        link(dve.reciprocal(rden[at], den[at]))
                        link(dve.tensor_tensor(coef[at], rden[at], s_[9][:, :, e], ALU.mult))
                        dve.tensor_tensor(mixed[s][:, :, e * HD:(e + 1) * HD],
                                          tile[:, 0:SEQS * HD].rearrange("p (b d) -> p b d", b=SEQS),
                                          coef[at].unsqueeze(2).broadcast_to([P, SEQS, HD]), ALU.mult).then_inc(freed, 1)
                        yield
                    yield
                    residual(("proj", s), s)

                def heads(s):
                    for p in range(2):
                        emptied(("proj", s, p))
                    yield from norm(s, L + 1)
                    for slot in range(5):
                        yield
                    maxima(("score1", s, 0), s, E, DH ** -0.5)
                    yield
                    for a in range(H):
                        t = E + a
                        if a + 1 < H:
                            maxima(("score1", s, a + 1), s, t + 1, DH ** -0.5)
                        yield
                        tile, freed = take(("av1", s, a))
                        at = (slice(None), s, t % 2)
                        link(dve.reciprocal(rden[at], den[at]))
                        dve.tensor_tensor(mixed[s][:, :, a * DH:(a + 1) * DH],
                                          tile[:, 0:SEQS * DH].rearrange("p (b d) -> p b d", b=SEQS),
                                          rden[at].unsqueeze(2).broadcast_to([P, SEQS, DH]), ALU.mult).then_inc(freed, 1)
                        yield
                    yield
                    residual(("proj1", s), s)

                def mlp(s):
                    for p in range(2):
                        emptied(("proj1", s, p))
                    yield from norm(s, L + 2)
                    for slot in range(4):
                        yield
                    dve.wait_ge(stored, i * (16 * S) + (16 * s + 16))
                    for p in range(2):
                        tile, freed = take(("ffn", s, p))
                        dve.tensor_tensor(result[:, 2 * p:2 * p + 2, :], h[s][:, 2 * p:2 * p + 2, :],
                                          tile[:, 0:2 * C].rearrange("p (b c) -> p b c", b=2), ALU.add).then_inc(freed, 1)
                    yield

                phases(scan, post, norm, before, experts, heads, mlp)
                assert links[0] == DVE_LINKS, f"DVE_LINKS = {links[0]}"


_INS = {
    "ids": "x", "emb": "L0_tok_emb", "norm_w": "L0_tok_norm_w", "in_w": "L0_tok_in_proj_w",
    "conv_w": "L0_tok_conv_w", "conv_b": "L0_tok_conv_b", "x_w": "L0_tok_x_proj_w", "dt_w": "L0_tok_dt_proj_w",
    "dt_b": "L0_tok_dt_proj_b", "A_log": "L0_tok_A_log", "D": "L0_tok_D", "out_w": "L0_tok_out_proj_w",
    "in_w2": "L0_attn_W_in", "conv_w2": "L0_attn_conv_w", "conv_b2": "L0_attn_conv_b", "x_w2": "L0_attn_W_x",
    "dt_w2": "L0_attn_W_dt", "dt_b2": "L0_attn_b_dt", "A_log2": "L0_attn_A_log", "D2": "L0_attn_D",
    "out_w2": "L0_attn_W_out", "Wqk": "L0_ffn_Wqk", "bqk": "L0_ffn_bqk", "Wv": "L0_ffn_Wv", "bv": "L0_ffn_bv",
    "ec_w": "L0_ffn_conv_w", "ec_b": "L0_ffn_conv_b", "Wg1": "L0_ffn_Wg1", "bg1": "L0_ffn_bg1",
    "Wg2": "L0_ffn_Wg2", "bg2": "L0_ffn_bg2", "Wp": "L0_ffn_Wp", "bp": "L0_ffn_bp",
    "Wq": "L1_attn_Wq", "bq": "L1_attn_bq", "Wk": "L1_attn_Wk", "bk": "L1_attn_bk", "Wv1": "L1_attn_Wv",
    "bv1": "L1_attn_bv", "Wo": "L1_attn_Wo", "bo": "L1_attn_bo", "ffn_wi": "L1_ffn_in_weight",
    "ffn_bi": "L1_ffn_in_bias", "ffn_wo": "L1_ffn_out_weight",
}
_TRANSPOSED = ("ids", "ffn_wi")


def kernel(**inputs):
    import numpy as _np
    import concourse.bacc as _bacc
    from concourse import mybir as _mybir
    from concourse.bass_utils import run_bass_kernel_spmd as _run

    nc = _bacc.Bacc("TRN2", target_bir_lowering=False, num_devices=1)
    arrays, A = {}, {}
    for name, given in _INS.items():
        a = _np.asarray(inputs[given])
        a = _np.ascontiguousarray(a.T if name in _TRANSPOSED else a)
        arrays[f"in_{name}_dram"] = a
        A[name] = nc.dram_tensor(f"in_{name}_dram", a.shape, _mybir.dt.from_np(a.dtype), kind="ExternalInput").ap()
    out = nc.dram_tensor("out_0_dram", (128, 128, 192), _mybir.dt.float32, kind="ExternalOutput").ap()
    scratch = nc.dram_tensor("bc_dram", (2, 2, 16, 512), _mybir.dt.float32, kind="Internal").ap()
    tower(nc, A, out, scratch)
    r = _run(nc, [arrays], core_ids=[0])
    return r.results[0]["out_0_dram"]
```

```python
from contextlib import ExitStack

import concourse.bass as bass
from concourse import mybir

F32, BF16 = mybir.dt.float32, mybir.dt.bfloat16
U32 = mybir.dt.uint32
ALU, ACT, AX = mybir.AluOpType, mybir.ActivationFunctionType, mybir.AxisListType

P = 128
EPS = 1e-5
MASKED = -3.0e38
LARGEST_LOG = 80.0
EXP_SET = "natural_log_exp_and_others"

DVE_LINKS = (14, 188)
ACT_LINKS = (1, 6)


def nth(i, per, k):
    return i * per + (k + 1)


def side_by_side(*tasks):
    tasks = list(tasks)
    while tasks:
        tasks = [task for task in tasks if next(task, "ended") != "ended"]


def lasting(slots, task):
    for slot in range(slots):
        next(task, None)
        yield
    assert next(task, "ended") == "ended"


def tower(nc, A, out, scratch):
    B, T = 128, 128
    V, C = A["emb"].shape
    SEQS = 4
    S = 2
    ROUNDS = B // (SEQS * S)
    N = SEQS * T
    KC, CH = 96, C // 96
    DI = A["out_w"].shape[1]
    MB = DI // P
    L = 3
    NS = A["A_log"].shape[2]
    R = A["dt_w"].shape[1]
    XD = R + 2 * NS
    SCANS = S * L
    BUFS = 4
    ROWS_B = 4
    DECAYS = 3
    SIDE = 2
    E, HD = 3, 64
    H, DH, HG = 12, 16, 4
    HGS = H // HG
    HID = A["ffn_wi"].shape[1]
    FB = HID // P
    STAGES = L + 3
    UNITS = 4
    GATHER = 16 * SEQS
    BANKS = SIDE + MB
    FIRST = CH + 3 * MB + 1
    SCORES = (S - 1) * E + S * H
    SIDES = S * (STAGES * CH + L * (2 * MB + 1 + MB + 2) + (2 + 4 + 2 + 3 * E + CH + 2)
                 + (2 * HGS + 2 + 3 * H + CH + 2) + (FB + 2)) - SCORES
    per_bank = [len(range(x, SIDES, SIDE)) for x in range(SIDE)] + [SCORES // MB] * MB
    assert SCORES % MB == 0 and FIRST % SIDE == 0
    places = {"first": {}, "loop": {}}
    with ExitStack() as ctx:
        def sb(name, shape, dt=F32):
            return ctx.enter_context(nc.sbuf_tensor(name, shape, dt))

        primed = []

        def sem(name, prime=True):
            s = ctx.enter_context(nc.semaphore(name))
            if prime:
                primed.append(s)
            return s

        in_w = sb("in_w", [KC, L, CH, 2 * DI])
        norm_w = sb("norm_w", [KC, 2, CH])
        conv_w = sb("conv_w", [P, L, MB, 4])
        conv_b = sb("conv_b", [P, L, MB])
        x_w = sb("x_w", [P, L, MB, XD])
        dt_w = sb("dt_w", [R, L, DI])
        dt_b = sb("dt_b", [P, L, MB])
        decay = sb("decay", [P, L, MB, NS])
        skip = sb("skip", [P, L, MB])
        out_w = sb("out_w", [P, L, MB, C])
        gate1_w = sb("gate1_w", [KC, CH, 32])
        gate1_b = sb("gate1_b", [32, 1])
        gate2_w = sb("gate2_w", [32, E])
        gate2_b = sb("gate2_b", [1, E])
        qk_w = sb("qk_w", [KC, CH, 2 * C])
        qk_b = sb("qk_b", [P, 4])
        ev_w = sb("ev_w", [KC, CH, C])
        ev_b = sb("ev_b", [1, C])
        ec_w = sb("ec_w", [HD, 3])
        ec_b = sb("ec_b", [HD, 1])
        ep_w = sb("ep_w", [KC, CH, C])
        ep_b = sb("ep_b", [1, C])
        q_w = sb("q_w", [KC, CH, H, 32])
        k_w = sb("k_w", [KC, CH, H, 32])
        q_b = sb("q_b", [P, HGS])
        k_b = sb("k_b", [P, HGS])
        v_w = sb("v_w", [KC, CH, C])
        v_b = sb("v_b", [1, C])
        o_w = sb("o_w", [KC, CH, C])
        o_b = sb("o_b", [1, C])
        ffn_wi = sb("ffn_wi_sb", [KC, CH, HID])
        ffn_bi = sb("ffn_bi_sb", [P, FB])
        ffn_wo = sb("ffn_wo_sb", [P, FB, C])
        ident = sb("ident", [P, P])
        identb = sb("identb", [P, P], BF16)
        causal = sb("causal", [P, SEQS, P], BF16)
        ones = sb("ones", [1, P])
        power = sb("power", [P, SEQS])
        rows = sb("rows", [P, B + SEQS * S], U32)
        rows_now = sb("rows_now", [P, S, SEQS], U32)
        h = [sb(f"h{s}", [P, SEQS, C]) for s in range(S)]
        result = sb("result", [P, SEQS, C])
        xn = [sb(f"xn{s}", [P, SEQS, C]) for s in range(S)]
        stats = sb("stats", [P, S, SEQS, 6])
        mean_var = sb("mean_var", [P, S, SEQS, 2])
        mean_sq = sb("mean_sq", [P, S, SEQS])
        var = sb("var", [P, S, SEQS])
        rstd = sb("rstd", [P, S, SEQS])
        xT = [sb(f"xT{s}", [KC, CH, N]) for s in range(S)]
        arena = [sb(f"arena{s}", [P, 5, MB * N]) for s in range(S)]

        def part(a, s, m):
            return arena[s][:, a, :].rearrange("p (m n) -> p m n", m=m)

        conv, u, gate, delta, w = ([part(a, s, MB) for s in range(S)] for a in range(5))
        soft_e, soft_l, soft_r, y = conv, delta, w, conv
        x_dbl = [sb(f"x_dbl{s}", [XD, N]) for s in range(S)]
        bc = [sb(f"bc{x}", [P, 2, N]) for x in range(ROWS_B)]
        state = [sb(f"state{x}", [P, MB, N]) for x in range(BUFS)]
        ids = state[0][:, 0, 0:B].bitcast(mybir.dt.int32)
        idf, wrap = state[0][:, 1, 0:B], state[0][:, 2, 0:B]
        g1 = [sb(f"g1_{s}", [32, N]) for s in range(S)]
        small = sb("small", [P, S, 16, SEQS, E])
        small1 = sb("small1", [P, S, 4, SEQS])
        q01, k01, q2 = ([part(0, s, 3)[:, m, :] for s in range(S)] for m in range(3))
        k2, qc = ([part(1, s, 3)[:, m, :] for s in range(S)] for m in range(2))
        vv, mixed = ([arena[s][:, 2, x * SEQS * C:(x + 1) * SEQS * C].rearrange("p (b c) -> p b c", b=SEQS)
                      for s in range(S)] for x in range(2))
        probs, probsT = ([[part(a, s, 3)[:, x, :].rearrange("p (b k) -> p b k", k=P) for x in range(2)]
                          for s in range(S)] for a in (3, 4))
        neg_max, row_max, den, rden, coef = (sb(name, [P, S, UNITS, SEQS])
                                             for name in ("neg_max", "row_max", "den", "rden", "coef"))
        qT, kT = ([part(a, s, HGS) for s in range(S)] for a in range(2))
        hid = [arena[s][:, 3:5, :].rearrange("p a (m n) -> p (a m) n", n=N) for s in range(S)]

        dA = [ctx.enter_context(nc.psum_tensor(f"dA{x}", [P, N], F32)) for x in range(DECAYS)]
        y_sum = [ctx.enter_context(nc.psum_tensor(f"y_sum{d}", [P, N], F32)) for d in range(MB)]
        bank = [ctx.enter_context(nc.psum_tensor(f"side{x}", [P, 512], F32)) for x in range(SIDE)] + y_sum

        loaded = sem("loaded", False)
        ids_loaded = sem("ids_loaded", False)
        gathered = [sem(f"gathered{s}", False) for s in range(S)]
        stored = sem("stored", False)
        bc_stored = [sem(f"bc_stored{s}", False) for s in range(S)]
        bc_loaded = [sem(f"bc_loaded{x}", False) for x in range(ROWS_B)]
        consts = sem("consts", False)
        consts_dve = sem("consts_dve", False)
        log_a_capped = sem("log_a_capped", False)
        log_a = sem("log_a", False)
        set_up = sem("set_up", False)
        rows_ready = sem("rows_ready", False)
        rows_picked = sem("rows_picked", False)
        gate_pool = sem("gate_pool", False)
        gate_dve = sem("gate_dve", False)
        gate_sp = sem("gate_sp", False)
        full = [sem(f"full{x}") for x in range(BANKS)]
        free = [sem(f"free{x}") for x in range(BANKS)]

        def each(name):
            return [sem(f"{name}{s}") for s in range(S)]

        var_ready, rstd_ready, xn_ready = each("var_ready"), each("rstd_ready"), each("xn_ready")
        u_ready, gate_in, gate_ready = each("u_ready"), each("gate_in"), each("gate_ready")
        abs_ready, soft_ready, delta_ready, w_ready = each("abs_ready"), each("soft_ready"), each("delta_ready"), each("w_ready")
        y_ready = each("y_ready")
        top_in, top_out, qc_ready, max_ready = each("top_in"), each("top_out"), each("qc_ready"), each("max_ready")
        hid_ready = each("hid_ready")
        exp_ready = sem("exp_ready")
        input_ready = sem("input_ready")
        scanned = sem("scanned")
        weighed = sem("weighed")
        summed = sem("summed")
        y_free = sem("y_free")
        dve_link = sem("dve_link")
        act_link = sem("act_link")

        weights = [
            (in_w[:, 0:2], A["in_w"].rearrange("l (k p) n -> p l k n", p=KC)),
            (in_w[:, 2], A["in_w2"].rearrange("(k p) n -> p k n", p=KC)),
            (norm_w[:], A["norm_w"].rearrange("l (k p) -> p l k", p=KC)),
            (conv_w[:, 0:2], A["conv_w"].rearrange("l (m p) o k -> p l m (o k)", p=P)),
            (conv_w[:, 2], A["conv_w2"].rearrange("(m p) o k -> p m (o k)", p=P)),
            (conv_b[:, 0:2], A["conv_b"].rearrange("l (m p) -> p l m", p=P)),
            (conv_b[:, 2], A["conv_b2"].rearrange("(m p) -> p m", p=P)),
            (x_w[:, 0:2], A["x_w"].rearrange("l (m p) n -> p l m n", p=P)),
            (x_w[:, 2], A["x_w2"].rearrange("(m p) n -> p m n", p=P)),
            (dt_w[:, 0:2], A["dt_w"].rearrange("l r n -> r l n")),
            (dt_w[:, 2], A["dt_w2"]),
            (dt_b[:, 0:2], A["dt_b"].rearrange("l (m p) -> p l m", p=P)),
            (dt_b[:, 2], A["dt_b2"].rearrange("(m p) -> p m", p=P)),
            (decay[:, 0:2], A["A_log"].rearrange("l (m p) n -> p l m n", p=P)),
            (decay[:, 2], A["A_log2"].rearrange("(m p) n -> p m n", p=P)),
            (skip[:, 0:2], A["D"].rearrange("l (m p) -> p l m", p=P)),
            (skip[:, 2], A["D2"].rearrange("(m p) -> p m", p=P)),
            (out_w[:, 0:2], A["out_w"].rearrange("l (m p) n -> p l m n", p=P)),
            (out_w[:, 2], A["out_w2"].rearrange("(m p) n -> p m n", p=P)),
            (gate1_w[:], A["Wg1"].rearrange("(k p) n -> p k n", p=KC)),
            (gate1_b[:], A["bg1"].rearrange("(p o) -> p o", o=1)),
            (gate2_w[:], A["Wg2"]),
            (gate2_b[:], A["bg2"].rearrange("(o p) -> o p", o=1)),
            (qk_w[:], A["Wqk"].rearrange("(k p) n -> p k n", p=KC)),
            (qk_b[:, 0:1], A["bqk"][0:P].rearrange("(p o) -> p o", o=1)),
            (qk_b[:, 1:2], A["bqk"][C:C + P].rearrange("(p o) -> p o", o=1)),
            (qk_b[0:HD, 2:3], A["bqk"][P:C].rearrange("(p o) -> p o", o=1)),
            (qk_b[0:HD, 3:4], A["bqk"][C + P:2 * C].rearrange("(p o) -> p o", o=1)),
        ] + [
            (ev_w[:, :, e * HD:(e + 1) * HD], A["Wv"][e].rearrange("(k p) d -> p k d", p=KC)) for e in range(E)
        ] + [
            (ev_b[:], A["bv"].rearrange("(o e) d -> o (e d)", o=1)),
            (ec_w[:], A["ec_w"].rearrange("p o k -> p (o k)")),
            (ec_b[:], A["ec_b"].rearrange("(p o) -> p o", o=1)),
            (ep_w[:], A["Wp"].rearrange("(k p) n -> p k n", p=KC)),
            (ep_b[:], A["bp"].rearrange("(o p) -> o p", o=1)),
            (v_w[:], A["Wv1"].rearrange("(k p) n -> p k n", p=KC)),
            (v_b[:], A["bv1"].rearrange("(o p) -> o p", o=1)),
            (o_w[:], A["Wo"].rearrange("(k p) n -> p k n", p=KC)),
            (o_b[:], A["bo"].rearrange("(o p) -> o p", o=1)),
            (ffn_wi[:], A["ffn_wi"].rearrange("(k p) n -> p k n", p=KC)),
            (ffn_bi[:], A["ffn_bi"].rearrange("(m p) -> p m", p=P)),
            (ffn_wo[:], A["ffn_wo"].rearrange("(m p) n -> p m n", p=P)),
        ]
        padded = []
        for to, name in ((q_w, "Wq"), (k_w, "Wk")):
            for k in range(CH):
                padded.append((to[:, k, :, 0:DH],
                               A[name][k * KC:(k + 1) * KC].rearrange("p (h c) -> p h c", c=DH)))
        for to, name in ((q_b, "bq"), (k_b, "bk")):
            for j in range(HG):
                padded.append((to[32 * j:32 * j + DH, :],
                               A[name].rearrange("(g j c) -> j c g", j=HG, c=DH)[j]))
        LOADED = 16 * (len(weights) + len(padded))

        ctx.enter_context(nc.allow_non_contiguous_dma(reason="small vectors, loaded once"))
        block = ctx.enter_context(nc.Block())

        def chunk(s, l, n):
            return (l * S + s) * NS + n

        def phases(part_, scan, post, norm, before, experts, heads, mlp, scan_last=False):
            def beside(*tasks):
                side_by_side(*(reversed(tasks) if scan_last else tasks))

            def onward(s, l, ahead=0):
                if l:
                    yield from post(s, l - 1)
                yield from norm(s, l, ahead)
                yield
                yield from (before(s, l, ahead) if l < L else experts(s))

            def to_the_next():
                yield from lasting(24, heads(0))
                yield from lasting(7, mlp(0))
                yield from lasting(13, onward(0, 0, ahead=1))

            def to_the_end():
                yield from lasting(18, onward(1, L))
                yield from lasting(24, heads(1))
                yield from lasting(7, mlp(1))

            if part_ == "first":
                side_by_side(onward(0, 0))
                return
            for l in range(L):
                beside(scan(0, l), onward(1, l))
                beside(scan(1, l), onward(0, l + 1))
            side_by_side(to_the_next(), to_the_end())

        @block.tensor
        def _(pe):
            pe.wait_ge(set_up, 1)
            pe.wait_ge(consts, 2)
            placed = {"side": 0, "scores": 0}

            def program(part_, i):
                place = places[part_]
                waited = [0] * BANKS

                def wait_free(x, tiles):
                    if tiles > waited[x] or not tiles:
                        pe.wait_ge(free[x], nth(i, per_bank[x], tiles))
                    waited[x] = max(tiles, waited[x])

                def fill(name):
                    x, k = place[name] = placed["side"] % SIDE, placed["side"] // SIDE
                    placed["side"] += 1
                    wait_free(x, k)
                    return bank[x], full[x]

                def fill_sum(name):
                    x, k = place[name] = SIDE + placed["scores"] % MB, placed["scores"] // MB
                    placed["scores"] += 1
                    wait_free(x, k)
                    return bank[x], full[x]

                def emptied(name):
                    x, k = place[name]
                    wait_free(x, k + 1)

                def turn(name, src):
                    for k in range(CH):
                        tile, filled = fill(name + (k,))
                        for b in range(SEQS):
                            ins = pe.transpose(tile[0:KC, b * T:(b + 1) * T], src[:, b, k * KC:(k + 1) * KC], ident[:, :])
                        ins.then_inc(filled, 1)

                def from_xT(name, s, weight, m):
                    tile, filled = fill(name)
                    for k in range(CH):
                        ins = pe.matmul(tile[0:m, :], weight(k), xT[s][:, k, :], start=k == 0, stop=k == CH - 1)
                    ins.then_inc(filled, 1)

                def to_tokens(name, s, weight, bias):
                    for p in range(2):
                        tile, filled = fill(name + (p,))
                        for b in range(2 * p, 2 * p + 2):
                            to = tile[:, (b % 2) * C:(b % 2 + 1) * C]
                            for k in range(CH):
                                pe.matmul(to, xT[s][:, k, b * T:(b + 1) * T], weight[:, k, :], start=k == 0, stop=False)
                            ins = pe.matmul(to, ones[:, :], bias[:, :], start=False, stop=True)
                        ins.then_inc(filled, 1)

                def scan(s, l):
                    yield
                    yield
                    for n in range(NS):
                        Q = chunk(s, l, n)
                        pe.wait_ge(weighed, nth(i, SCANS * NS, Q + 1))
                        for d in range(MB):
                            if n == 0 and l == s == 0:
                                wait_free(SIDE + d, 0)
                            if n == 0:
                                pe.wait_ge(y_free, nth(i, SCANS * MB, (l * S + s - 1) * MB + d + 1 if l or s else 0))
                            ins = pe.matmul(y_sum[d][:, :], ident[:, :], state[Q % BUFS][:, d, :],
                                            start=n == 0, stop=n == NS - 1)
                        ins.then_inc(summed, 1)
                        yield

                def post(s, l):
                    yield
                    pe.wait_ge(y_ready[s], nth(i, L, l + 1))
                    for p in range(2):
                        tile, filled = fill(("out", s, l, p))
                        for b in range(2 * p, 2 * p + 2):
                            for m in range(MB):
                                ins = pe.matmul(tile[:, (b % 2) * C:(b % 2 + 1) * C], y[s][:, m, b * T:(b + 1) * T],
                                                out_w[:, l, m, :], start=m == 0, stop=m == MB - 1)
                        ins.then_inc(filled, 1)
                    yield

                def norm(s, stage, ahead=0):
                    yield
                    yield
                    pe.wait_ge(xn_ready[s], nth(i, STAGES, ahead * STAGES + stage + 1))
                    turn(("xT", s, stage), xn[s])

                def turned(s, stage):
                    for k in range(CH):
                        emptied(("xT", s, stage, k))

                def before(s, l, ahead=0):
                    turned(s, l)

                    def inner(m):
                        from_xT(("in", s, l, m), s, lambda k: in_w[:, l, k, m * P:(m + 1) * P], P)

                    for slot in range(MB + 1):
                        if slot < MB:
                            inner(slot)
                        if slot:
                            inner(MB + slot - 1)
                        yield
                    tile, filled = fill(("x", s, l))
                    pe.wait_ge(u_ready[s], nth(i, L, ahead * L + l + 1))
                    for m in range(MB):
                        ins = pe.matmul(tile[0:XD, :], x_w[:, l, m, :], u[s][:, m, :], start=m == 0, stop=m == MB - 1)
                    ins.then_inc(filled, 1)
                    yield
                    emptied(("x", s, l))
                    for m in range(MB):
                        tile, filled = fill(("dt", s, l, m))
                        pe.matmul(tile[:, :], dt_w[:, l, m * P:(m + 1) * P], x_dbl[s][0:R, :],
                                  start=True, stop=True).then_inc(filled, 1)
                        if m == 1:
                            yield
                    yield
                    yield
                    yield

                def turn_probs(name, score, s, t):
                    emptied(score)
                    tile, filled = fill(name)
                    for b in range(SEQS):
                        ins = pe.transpose(tile[:, b * P:(b + 1) * P], probs[s][t % 2][:, b, :], ident[:, :])
                    ins.then_inc(filled, 1)

                def weighted_values(name, turned_probs, s, t, first, width):
                    emptied(turned_probs)
                    tile, filled = fill(name)
                    for b in range(SEQS):
                        ins = pe.matmul(tile[:, b * width:(b + 1) * width], probsT[s][t % 2][:, b, :],
                                        vv[s][:, b, first:first + width], start=True, stop=True)
                    ins.then_inc(filled, 1)

                def attend(s, count, tag, t0, width, lead, scores):
                    for q in range(count + 2 + lead):
                        if lead and q < count:
                            scores(q)
                        a = q - 1 - lead
                        if 0 <= a < count:
                            turn_probs(("pT" + tag, s, a), ("score" + tag, s, a), s, t0 + a)
                        a = q - 2 - lead
                        if 0 <= a < count:
                            weighted_values(("av" + tag, s, a), ("pT" + tag, s, a), s, t0 + a, a * width, width)
                        if not lead and q < count:
                            scores(q)
                        yield

                def experts(s):
                    turned(s, L)
                    from_xT(("gate", s, 0), s, lambda k: gate1_w[:, k, :], 32)
                    yield
                    emptied(("gate", s, 0))
                    tile, filled = fill(("gate", s, 1))
                    for b in range(SEQS):
                        to = tile[:, b * E:(b + 1) * E]
                        pe.matmul(to, g1[s][:, b * T:(b + 1) * T], gate2_w[:, :], start=True, stop=False)
                        ins = pe.matmul(to, ones[:, :], gate2_b[:, :], start=False, stop=True)
                    ins.then_inc(filled, 1)
                    yield
                    for m, (first, parts) in enumerate(((0, P), (C, P), (P, HD), (C + P, HD))):
                        from_xT(("qk", s, m), s, lambda k: qk_w[:, k, first:first + parts], parts)
                        if m % 2:
                            yield
                    to_tokens(("v", s), s, ev_w, ev_b)
                    yield

                    def expert_scores(e):
                        tile, filled = (fill_sum if s else fill)(("score", s, e))
                        pe.matmul(tile[:, :], identb[:, :], causal[:, :, :].rearrange("p b k -> p (b k)"),
                                  start=True, stop=False, skip_group_check=True)
                        q_, k_ = ((qc[s][0:HD], k01[s][0:HD]), (q01[s][HD:P], k01[s][HD:P]), (q2[s][0:HD], k2[s][0:HD]))[e]
                        for b in range(SEQS):
                            at = slice(b * T, (b + 1) * T)
                            ins = pe.matmul(tile[:, at], q_[:, at], k_[:, at], start=False, stop=True, skip_group_check=True)
                        ins.then_inc(filled, 1)

                    pe.wait_ge(qc_ready[s], nth(i, 1, 1))
                    for p in range(2):
                        emptied(("v", s, p))
                    yield from attend(s, E, "", 0, HD, s, expert_scores)
                    emptied(("av", s, E - 1))
                    turn(("yT", s), mixed[s])
                    yield
                    for k in range(CH):
                        emptied(("yT", s, k))
                    to_tokens(("proj", s), s, ep_w, ep_b)

                def heads(s):
                    yield from norm(s, L + 1)
                    yield
                    turned(s, L + 1)
                    for x in range(2 * HGS):
                        g, weight = x % HGS, (q_w, k_w)[x // HGS]
                        from_xT(("q", s, x), s, lambda k: weight[:, k, g * HG:(g + 1) * HG, :].rearrange("p h c -> p (h c)"), P)
                        if x % 2:
                            yield
                    to_tokens(("v1", s), s, v_w, v_b)
                    yield

                    def head_scores(a):
                        rows_, g = slice(32 * (a % HG), 32 * (a % HG) + 32), a // HG
                        tile, filled = fill_sum(("score1", s, a))
                        for b in range(SEQS):
                            at = slice(b * T, (b + 1) * T)
                            ins = pe.matmul(tile[:, at], qT[s][rows_, g, at], kT[s][rows_, g, at], start=True, stop=True)
                        ins.then_inc(filled, 1)

                    for p in range(2):
                        emptied(("v1", s, p))
                    yield from attend(s, H, "1", E, DH, 1, head_scores)
                    emptied(("av1", s, H - 1))
                    turn(("yT1", s), mixed[s])
                    yield
                    for k in range(CH):
                        emptied(("yT1", s, k))
                    to_tokens(("proj1", s), s, o_w, o_b)

                def mlp(s):
                    yield from norm(s, L + 2)
                    yield
                    turned(s, L + 2)
                    for m in range(FB):
                        from_xT(("hid", s, m), s, lambda k: ffn_wi[:, k, m * P:(m + 1) * P], P)
                        if m % 2:
                            yield
                    pe.wait_ge(hid_ready[s], nth(i, 1, 1))
                    for p in range(2):
                        tile, filled = fill(("ffn", s, p))
                        for b in range(2 * p, 2 * p + 2):
                            for m in range(FB):
                                ins = pe.matmul(tile[:, (b % 2) * C:(b % 2 + 1) * C], hid[s][:, m, b * T:(b + 1) * T],
                                                ffn_wo[:, m, :], start=m == 0, stop=m == FB - 1)
                        ins.then_inc(filled, 1)
                    yield

                phases(part_, scan, post, norm, before, experts, heads, mlp, scan_last=True)

            program("first", 0)
            with pe.Fori(0, ROUNDS) as i:
                program("loop", i)
            assert len(places["first"]) == FIRST and placed["side"] == FIRST + SIDES and placed["scores"] == SCORES

        @block.sync
        def _(sp):
            for x in primed:
                sp.sem_inc(x, 1)
            sp.sem_inc(stored, 16)
            sp.dma_start(ids, A["ids"]).then_inc(ids_loaded, 16)
            for to, src in weights:
                sp.dma_start(to, src).then_inc(loaded, 16)
            sp.wait_ge(consts_dve, 1)
            for to, src in padded:
                sp.dma_start(to, src).then_inc(loaded, 16)
            def program(part_, i):
                place = places[part_]

                def scan(s, l):
                    for n in range(NS):
                        Q = chunk(s, l, n)
                        if n == 0:
                            sp.wait_ge(bc_stored[s], i * (16 * L) + 16 * (l + 1))
                            sp.sem_inc(gate_sp, 1)
                        sp.wait_ge(weighed, nth(i, SCANS * NS, max(Q - ROWS_B + 1, 0)))
                        sp.sem_inc(gate_sp, 1)
                        sp.dma_start(bc[Q % ROWS_B][:, :, :], scratch[s:s + 1, :, n, :].broadcast_to([P, 2, N])
                                     ).then_inc(bc_loaded[Q % ROWS_B], 16)
                        yield

                def post(s, l):
                    yield
                    yield

                def norm(s, stage, ahead=0):
                    yield
                    yield

                def before(s, l, ahead=0):
                    for slot in range(5):
                        yield
                    x, k = place[("x", s, l)]
                    sp.wait_ge(free[x], nth(i, per_bank[x], k + 1))
                    sp.sem_inc(gate_sp, 1)
                    sp.dma_start(scratch[s].rearrange("a n t -> (a n) t"), x_dbl[s][R:XD, :]).then_inc(bc_stored[s], 16)

                def experts(s):
                    yield

                def heads(s):
                    yield

                def mlp(s):
                    for slot in range(6):
                        yield
                    for p in range(2):
                        x, k = place[("ffn", s, p)]
                        sp.wait_ge(free[x], nth(i, per_bank[x], k + 1))
                        sp.sem_inc(gate_sp, 1)
                    sp.dma_start(out.rearrange("(g b) t c -> g t b c", b=SEQS)[i * S + s], result[:, :, :]).then_inc(stored, 16)

                phases(part_, scan, post, norm, before, experts, heads, mlp)

            program("first", 0)
            with sp.Fori(0, ROUNDS) as i:
                program("loop", i)
            sp.wait_ge(stored, 16 * S * ROUNDS + 16)
            for s in range(S):
                sp.wait_ge(bc_stored[s], 16 * (L * ROUNDS + (s == 0)))

        @block.gpsimd
        def _(pool):
            pool.memset(ident[:, :], 0.0)
            pool.memset(identb[:, :], 0.0)
            pool.memset(causal[:, :, :], 0.0)
            pool.memset(ones[:, :], 1.0)
            pool.memset(power[:, :], -0.5)
            pool.memset(rows[:, B:B + SEQS * S], 0).then_inc(consts, 1)
            pool.wait_ge(consts, 1)
            pool.affine_select(out=ident[:, :], in_=ident[:, :], compare_op=ALU.not_equal, fill=1.0,
                               base=0, pattern=[[-1, P]], channel_multiplier=1)
            pool.affine_select(out=identb[:, :], in_=identb[:, :], compare_op=ALU.not_equal, fill=1.0,
                               base=0, pattern=[[-1, P]], channel_multiplier=1)
            pool.affine_select(out=causal[:, :, :], in_=causal[:, :, :], compare_op=ALU.is_ge, fill=MASKED,
                               base=0, pattern=[[0, SEQS], [-1, P]], channel_multiplier=1).then_inc(consts, 1)

            def gather(s):
                for b in range(SEQS):
                    pool.indirect_dma_start(out=h[s][:, b, :], out_offset=None, in_=A["emb"][:, :],
                                            in_offset=bass.IndirectOffsetOnAxis(ap=rows_now[:, s, b:b + 1], axis=0)
                                            ).then_inc(gathered[s], 16)

            pool.wait_ge(rows_ready, 1)
            pool.tensor_copy(rows_now[:, :, :], rows[:, 0:S * SEQS].rearrange("p (s b) -> p s b", s=S)).then_inc(rows_picked, 1)
            pool.wait_ge(rows_picked, 1)
            for s in range(S):
                gather(s)
            def program(part_, i):
                place = places[part_]

                def scan(s, l):
                    for n in range(NS):
                        Q = chunk(s, l, n)
                        if n == 0:
                            pool.wait_ge(w_ready[s], nth(i, L, l + 1))
                        pool.wait_ge(bc_loaded[Q % ROWS_B], i * (16 * SCANS * NS // ROWS_B) + 16 * (Q // ROWS_B + 1))
                        pool.wait_ge(summed, nth(i, SCANS * NS, max(Q - BUFS + 1, 0)))
                        pool.tensor_tensor(state[Q % BUFS][:, :, :], w[s][:, :, :],
                                           bc[Q % ROWS_B][:, 0:1, :].broadcast_to([P, MB, N]), ALU.mult).then_inc(input_ready, 1)
                        yield

                def post(s, l):
                    yield
                    yield

                def norm(s, stage, ahead=0):
                    pool.wait_ge(var_ready[s], nth(i, STAGES, ahead * STAGES + stage + 1))
                    pool.tensor_tensor(rstd[:, s, :], var[:, s, :], power[:, :], ALU.pow).then_inc(rstd_ready[s], 1)
                    yield
                    yield

                def before(s, l, ahead=0):
                    for slot in range(9):
                        yield
                    pool.wait_ge(delta_ready[s], nth(i, L, ahead * L + l + 1))
                    pool.tensor_tensor(w[s][:, :, :], delta[s][:, :, :], u[s][:, :, :], ALU.mult).then_inc(w_ready[s], 1)

                def experts(s):
                    yield

                def heads(s):
                    yield from norm(s, L + 1)

                def mlp(s):
                    yield from norm(s, L + 2)
                    for slot in range(4):
                        yield
                    for p in range(2):
                        x, k = place[("ffn", s, p)]
                        pool.wait_ge(free[x], nth(i, per_bank[x], k + 1))
                    pool.tensor_copy(rows_now[:, s, :], rows[:, bass.ds((i + 1) * (SEQS * S) + s * SEQS, SEQS)]
                                     ).then_inc(rows_picked, 1)
                    pool.wait_ge(rows_picked, i * S + (s + 2))
                    pool.sem_inc(gate_pool, 1)
                    gather(s)

                phases(part_, scan, post, norm, before, experts, heads, mlp)

            program("first", 0)
            with pool.Fori(0, ROUNDS) as i:
                program("loop", i)
            for s in range(S):
                pool.wait_ge(gathered[s], GATHER * (ROUNDS + 1))

        @block.scalar
        def _(act):
            act.wait_ge(loaded, LOADED)
            act.wait_ge(log_a_capped, 1)
            act.activation(decay[:, :, :, :], decay[:, :, :, :], ACT.Exp).then_inc(log_a, 1)
            act.wait_ge(set_up, 1)
            act.preload_act_table_set(EXP_SET)
            def program(part_, i):
                place = places[part_]

                links = [0 if part_ == "first" else ACT_LINKS[0]]

                def link(ins):
                    links[0] += 1
                    ins.then_inc(act_link, 1)
                    act.wait_ge(act_link, nth(i, ACT_LINKS[1], links[0]))

                def take(name):
                    x, k = place[name]
                    act.wait_ge(full[x], nth(i, per_bank[x], k + 1))
                    return bank[x], free[x]

                def emptied(name):
                    x, k = place[name]
                    act.wait_ge(free[x], nth(i, per_bank[x], k + 1))

                def copy(name, to, parts=P, func=ACT.Copy, **how):
                    tile, freed = take(name)
                    act.activation(to, tile[0:parts, :], func, **how).then_inc(freed, 1)

                def copy_values(name, s):
                    for p in range(2):
                        tile, freed = take(name + (p,))
                        act.activation(vv[s][:, 2 * p:2 * p + 2, :].rearrange("p b c -> p (b c)"),
                                       tile[:, 0:2 * C], ACT.Copy).then_inc(freed, 1)

                def scan(s, l):
                    for n in range(NS):
                        if n == 0:
                            act.wait_ge(delta_ready[s], nth(i, L, l + 1))
                        for d in range(MB):
                            X = chunk(s, l, n) * MB + d
                            act.wait_ge(scanned, nth(i, SCANS * NS * MB, max(X - DECAYS + 1, 0)))
                            act.activation(dA[X % DECAYS][:, :].rearrange("p (b t) -> p b t", t=T)[:, :, 1:T],
                                           delta[s][:, d, :].rearrange("p (b t) -> p b t", t=T)[:, :, 1:T],
                                           ACT.Exp, scale=decay[:, l, d, n:n + 1]).then_inc(exp_ready, 1)
                        yield

                def post(s, l):
                    yield
                    yield

                def norm(s, stage, ahead=0):
                    yield
                    yield
                    for k in range(CH):
                        copy(("xT", s, stage, k), xT[s][:, k, :], KC)

                def before(s, l, ahead=0):
                    yield
                    for m in range(MB):
                        copy(("in", s, l, MB + m), gate[s][:, m, :])
                        if m < MB - 1:
                            yield
                    for m in range(1, MB):
                        emptied(("in", s, l, m))
                    act.activation(u[s][:, :, :], conv[s][:, :, :], ACT.Silu).then_inc(u_ready[s], 1)
                    for m in range(2 * MB - 2, 2 * MB):
                        emptied(("in", s, l, m))
                    act.activation(gate[s][:, :, :], gate[s][:, :, :], ACT.Silu).then_inc(gate_ready[s], 1)
                    act.preload_act_table_set(EXP_SET)
                    yield
                    copy(("x", s, l), x_dbl[s][:, :], XD)
                    yield
                    for m in range(MB):
                        tile, freed = take(("dt", s, l, m))
                        bias = dt_b[:, l, m:m + 1]
                        act.activation(soft_r[s][:, m, :], tile[:, :], ACT.Relu, bias=bias)
                        act.activation(soft_e[s][:, m, :], tile[:, :], ACT.Abs, bias=bias).then_inc(freed, 1)
                        if m == 1:
                            yield
                    yield
                    for m in range(1, MB):
                        emptied(("dt", s, l, m))
                    link(act.activation(soft_e[s][:, :, :], soft_e[s][:, :, :], ACT.Exp, scale=-1.0))
                    act.activation(soft_l[s][:, :, :], soft_e[s][:, :, :], ACT.Ln, bias=1.0).then_inc(soft_ready[s], 1)
                    yield
                    yield

                def exps(name, s, t, scale):
                    tile, freed = take(name)
                    act.wait_ge(max_ready[s], nth(i, E + H, t + 1))
                    for b in range(SEQS):
                        ins = act.activation(probs[s][t % 2][:, b, :], tile[:, b * P:(b + 1) * P], ACT.Exp,
                                             bias=neg_max[:, s, t % UNITS, b:b + 1], scale=scale,
                                             accum_out=den[:, s, t % UNITS, b:b + 1])
                    ins.then_inc(freed, 1)

                def attend(s, count, tag, t0, width, lead):
                    for q in range(count + 2 + lead):
                        if lead and 0 <= q - 1 < count:
                            exps(("score" + tag, s, q - 1), s, t0 + q - 1, width ** -0.5)
                        a = q - 1 - lead
                        if 0 <= a < count:
                            copy(("pT" + tag, s, a), probsT[s][(t0 + a) % 2][:, :, :].rearrange("p b k -> p (b k)"))
                        if not lead and q < count:
                            exps(("score" + tag, s, q), s, t0 + q, width ** -0.5)
                        yield

                def experts(s):
                    copy(("gate", s, 0), g1[s][:, :], 32, ACT.Relu, bias=gate1_b[:, 0:1])
                    yield
                    act.wait_ge(top_in[s], nth(i, 2, 1))
                    act.activation(small[:, s, 1], small[:, s, 1], ACT.Exp).then_inc(top_out[s], 1)
                    yield
                    for m, (to, parts) in enumerate(((q01, P), (k01, P), (q2, HD), (k2, HD))):
                        copy(("qk", s, m), to[s][0:parts, :], parts, ACT.Identity, bias=qk_b[0:parts, m:m + 1])
                        if m == 1:
                            act.wait_ge(top_in[s], nth(i, 2, 2))
                            act.activation(small[:, s, 3], small[:, s, 3], ACT.Exp).then_inc(top_out[s], 1)
                        if m % 2:
                            yield
                    copy_values(("v", s), s)
                    yield
                    yield from attend(s, E, "", 0, HD, s)
                    for k in range(CH):
                        copy(("yT", s, k), xT[s][:, k, :], KC)
                    yield

                def heads(s):
                    yield from norm(s, L + 1)
                    yield
                    for x in range(2 * HGS):
                        g = x % HGS
                        to, bias = ((qT, q_b), (kT, k_b))[x // HGS]
                        copy(("q", s, x), to[s][:, g, :], P, ACT.Identity, bias=bias[:, g:g + 1])
                        if x % 2:
                            yield
                    copy_values(("v1", s), s)
                    yield
                    yield from attend(s, H, "1", E, DH, 1)
                    for k in range(CH):
                        copy(("yT1", s, k), xT[s][:, k, :], KC)
                    yield

                def mlp(s):
                    yield from norm(s, L + 2)
                    yield
                    for m in range(FB):
                        copy(("hid", s, m), hid[s][:, m, :], P, ACT.Identity, bias=ffn_bi[:, m:m + 1])
                        if m == FB - 1:
                            for x in range(FB - 2, FB):
                                emptied(("hid", s, x))
                            act.activation(hid[s][:, :, :], hid[s][:, :, :], ACT.Gelu).then_inc(hid_ready[s], 1)
                            act.preload_act_table_set(EXP_SET)
                        if m % 2:
                            yield
                    yield

                phases(part_, scan, post, norm, before, experts, heads, mlp)
                return links[0] - (0 if part_ == "first" else ACT_LINKS[0])

            first_links = program("first", 0)
            with act.Fori(0, ROUNDS) as i:
                loop_links = program("loop", i)
            assert (first_links, loop_links) == ACT_LINKS, f"ACT_LINKS = {first_links, loop_links}"

        @block.vector
        def _(dve):
            dve.memset(q_w[:, :, :, :], 0.0)
            dve.memset(k_w[:, :, :, :], 0.0)
            dve.memset(q_b[:, :], 0.0)
            dve.memset(k_b[:, :], 0.0).then_inc(consts_dve, 1)
            for x in range(DECAYS):
                dve.memset(dA[x][:, :].rearrange("p (b t) -> p b t", t=T)[:, :, 0:1], 0.0)
            dve.wait_ge(ids_loaded, 16)
            dve.tensor_copy(idf, ids).then_inc(consts_dve, 1)
            dve.wait_ge(consts_dve, 2)
            dve.tensor_scalar(wrap, idf, 0.0, float(V), ALU.is_lt, ALU.mult).then_inc(consts_dve, 1)
            dve.wait_ge(consts_dve, 3)
            dve.tensor_tensor(idf, idf, wrap, ALU.add).then_inc(consts_dve, 1)
            dve.wait_ge(consts_dve, 4)
            dve.tensor_scalar(rows[:, 0:B], idf, 0.0, float(V - 1), ALU.max, ALU.min).then_inc(rows_ready, 1)
            dve.wait_ge(loaded, LOADED)
            dve.tensor_scalar(decay[:, :, :, :], decay[:, :, :, :], LARGEST_LOG, None, ALU.min).then_inc(log_a_capped, 1)
            for l in range(2):
                for k in range(CH):
                    dve.tensor_scalar(in_w[:, l, k, :], in_w[:, l, k, :], norm_w[:, l, k:k + 1], None, ALU.mult)
            dve.wait_ge(log_a, 1)
            dve.tensor_scalar(decay[:, :, :, :], decay[:, :, :, :], -1.0, None, ALU.mult).then_inc(set_up, 1)
            dve.wait_ge(consts, 2)
            def program(part_, i):
                place = places[part_]

                links = [0 if part_ == "first" else DVE_LINKS[0]]

                def link(ins):
                    links[0] += 1
                    ins.then_inc(dve_link, 1)
                    dve.wait_ge(dve_link, nth(i, DVE_LINKS[1], links[0]))

                def take(name):
                    x, k = place[name]
                    dve.wait_ge(full[x], nth(i, per_bank[x], k + 1))
                    return bank[x], free[x]

                def emptied(name):
                    x, k = place[name]
                    dve.wait_ge(free[x], nth(i, per_bank[x], k + 1))

                def residual(name, s):
                    for p in range(2):
                        tile, freed = take(name + (p,))
                        dve.tensor_tensor(h[s][:, 2 * p:2 * p + 2, :], h[s][:, 2 * p:2 * p + 2, :],
                                          tile[:, 0:2 * C].rearrange("p (b c) -> p b c", b=2), ALU.add).then_inc(freed, 1)

                def scan(s, l):
                    def weigh(Q):
                        dve.wait_ge(scanned, nth(i, SCANS * NS * MB, (Q + 1) * MB))
                        dve.tensor_tensor(state[Q % BUFS][:, :, :], state[Q % BUFS][:, :, :],
                                          bc[Q % ROWS_B][:, 1:2, :].broadcast_to([P, MB, N]), ALU.mult).then_inc(weighed, 1)

                    for n in range(NS):
                        Q = chunk(s, l, n)
                        dve.wait_ge(bc_loaded[Q % ROWS_B], i * (16 * SCANS * NS // ROWS_B) + 16 * (Q // ROWS_B + 1))
                        dve.wait_ge(input_ready, nth(i, SCANS * NS, Q + 1))
                        for d in range(MB):
                            X = Q * MB + d
                            dve.wait_ge(exp_ready, nth(i, SCANS * NS * MB, X + 1))
                            dve.tensor_tensor_scan(out=state[Q % BUFS][:, d, :], data0=dA[X % DECAYS][:, :],
                                                   data1=state[Q % BUFS][:, d, :], initial=0.0,
                                                   op0=ALU.mult, op1=ALU.add).then_inc(scanned, 1)
                        if n:
                            weigh(Q - 1)
                        yield
                    weigh(chunk(s, l, NS - 1))

                def post(s, l):
                    dve.wait_ge(summed, nth(i, SCANS * NS, chunk(s, l, NS)))
                    dve.wait_ge(gate_ready[s], nth(i, L, l + 1))
                    for d in range(MB):
                        dve.scalar_tensor_tensor(out=y[s][:, d, :], in0=u[s][:, d, :], scalar=skip[:, l, d:d + 1],
                                                 in1=y_sum[d][:, :], op0=ALU.mult, op1=ALU.add).then_inc(y_free, 1)
                    dve.wait_ge(y_free, nth(i, SCANS * MB, (l * S + s + 1) * MB))
                    dve.tensor_tensor(y[s][:, :, :], y[s][:, :, :], gate[s][:, :, :], ALU.mult).then_inc(y_ready[s], 1)
                    yield
                    residual(("out", s, l), s)
                    for p in range(2):
                        emptied(("out", s, l, p))
                    yield

                def norm(s, stage, ahead=0):
                    if stage == 0:
                        dve.wait_ge(gathered[s], i * GATHER + (1 + ahead) * GATHER)
                    for b in range(SEQS):
                        ins = dve.bn_stats(stats[:, s, b, :], h[s][:, b, :])
                    link(ins)
                    dve.sem_inc(gate_dve, 1)
                    for b in range(SEQS):
                        ins = dve.bn_aggr(mean_var[:, s, b, :], stats[:, s, b, :])
                    link(ins)
                    if stage < 2:
                        link(dve.tensor_tensor(mean_sq[:, s, :], mean_var[:, s, :, 0], mean_var[:, s, :, 0], ALU.mult))
                        dve.scalar_tensor_tensor(out=var[:, s, :], in0=mean_sq[:, s, :], scalar=EPS, in1=mean_var[:, s, :, 1],
                                                 op0=ALU.add, op1=ALU.add).then_inc(var_ready[s], 1)
                    else:
                        dve.tensor_scalar(var[:, s, :], mean_var[:, s, :, 1], EPS, None, ALU.add).then_inc(var_ready[s], 1)
                    yield
                    dve.wait_ge(rstd_ready[s], nth(i, STAGES, ahead * STAGES + stage + 1))
                    for b in range(SEQS):
                        if stage < 2:
                            ins = dve.tensor_scalar(xn[s][:, b, :], h[s][:, b, :], rstd[:, s, b:b + 1], None, ALU.mult)
                        else:
                            ins = dve.tensor_scalar(xn[s][:, b, :], h[s][:, b, :], mean_var[:, s, b, 0:1], rstd[:, s, b:b + 1],
                                                    ALU.subtract, ALU.mult)
                    ins.then_inc(xn_ready[s], 1)
                    yield

                def before(s, l, ahead=0):
                    for m in range(MB):
                        tile, freed = take(("in", s, l, m))
                        x = tile[:, :].rearrange("p (b t) -> p b t", t=T)
                        acc = conv[s][:, m, :].rearrange("p (b t) -> p b t", t=T)
                        link(dve.tensor_scalar(acc, x, conv_w[:, l, m, 3:4], conv_b[:, l, m:m + 1], ALU.mult, ALU.add))
                        for lag in range(1, 4):
                            ins = dve.scalar_tensor_tensor(out=acc[:, :, lag:T], in0=x[:, :, 0:T - lag],
                                                           scalar=conv_w[:, l, m, 3 - lag:4 - lag],
                                                           in1=acc[:, :, lag:T], op0=ALU.mult, op1=ALU.add)
                            if lag < 3:
                                link(ins)
                        ins.then_inc(freed, 1)
                        yield
                    for slot in range(5):
                        yield
                    dve.wait_ge(soft_ready[s], nth(i, L, ahead * L + l + 1))
                    link(dve.scalar_tensor_tensor(out=soft_e[s][:, :, :], in0=soft_e[s][:, :, :], scalar=-2.0,
                                                  in1=soft_e[s][:, :, :], op0=ALU.add, op1=ALU.mult))
                    link(dve.scalar_tensor_tensor(out=soft_l[s][:, :, :], in0=soft_e[s][:, :, :], scalar=-0.5,
                                                  in1=soft_l[s][:, :, :], op0=ALU.mult, op1=ALU.max))
                    dve.tensor_tensor(delta[s][:, :, :], soft_l[s][:, :, :], soft_r[s][:, :, :], ALU.add).then_inc(delta_ready[s], 1)
                    yield

                def maxima(name, s, t, scale):
                    tile, freed = take(name)
                    at = (slice(None), s, t % UNITS)
                    link(dve.tensor_reduce(row_max[at], tile[:, :].rearrange("p (b k) -> p b k", k=P), AX.X, ALU.max))
                    dve.tensor_scalar(neg_max[at], row_max[at], -scale, None, ALU.mult).then_inc(max_ready[s], 1)

                def attend(s, count, tag, t0, width, lead, weights=None):
                    def normalise(a):
                        tile, freed = take(("av" + tag, s, a))
                        at = (slice(None), s, (t0 + a) % UNITS)
                        over = rden[at]
                        link(dve.reciprocal(rden[at], den[at]))
                        if weights is not None:
                            over = coef[at]
                            link(dve.tensor_tensor(coef[at], rden[at], weights[:, :, a], ALU.mult))
                        dve.tensor_tensor(mixed[s][:, :, a * width:(a + 1) * width],
                                          tile[:, 0:SEQS * width].rearrange("p (b d) -> p b d", b=SEQS),
                                          over.unsqueeze(2).broadcast_to([P, SEQS, width]), ALU.mult).then_inc(freed, 1)

                    for q in range(count + 2 + lead):
                        if lead and q < count:
                            maxima(("score" + tag, s, q), s, t0 + q, width ** -0.5)
                        if 0 <= q - 2 - lead < count:
                            normalise(q - 2 - lead)
                        if not lead and q < count:
                            maxima(("score" + tag, s, q), s, t0 + q, width ** -0.5)
                        yield

                def experts(s):
                    s_ = [small[:, s, x] for x in range(16)]
                    s1 = [small1[:, s, x] for x in range(4)]

                    def spread(x):
                        return x.unsqueeze(2).broadcast_to([P, SEQS, E])

                    yield
                    tile, freed = take(("gate", s, 1))
                    dve.tensor_copy(s_[0], tile[:, 0:SEQS * E].rearrange("p (b e) -> p b e", e=E)).then_inc(freed, 1)
                    emptied(("gate", s, 1))
                    link(dve.tensor_reduce(s1[0], s_[0], AX.X, ALU.max))
                    dve.tensor_tensor(s_[1], s_[0], spread(s1[0]), ALU.subtract).then_inc(top_in[s], 1)
                    yield
                    dve.wait_ge(top_out[s], nth(i, 2, 1))
                    link(dve.tensor_reduce(s1[1], s_[1], AX.X, ALU.add))
                    link(dve.reciprocal(s1[1], s1[1]))
                    link(dve.tensor_tensor(s_[2], s_[1], spread(s1[1]), ALU.mult))
                    link(dve.tensor_reduce(s1[2], s_[2], AX.X, ALU.max))
                    dve.tensor_tensor(s_[3], s_[2], spread(s1[2]), ALU.subtract).then_inc(top_in[s], 1)
                    yield
                    p0, p1, p2 = (s_[2][:, :, e] for e in range(E))
                    ge, lt, left = s_[4], s_[5], s_[6]
                    for x, (a, b) in enumerate(((p0, p1), (p0, p2), (p1, p2))):
                        dve.tensor_tensor(ge[:, :, x], a, b, ALU.is_ge)
                        ins = dve.tensor_tensor(lt[:, :, x], a, b, ALU.is_lt)
                    link(ins)
                    dve.tensor_tensor(left[:, :, 0], lt[:, :, 0], lt[:, :, 1], ALU.mult)
                    dve.tensor_tensor(left[:, :, 1], ge[:, :, 0], lt[:, :, 2], ALU.mult)
                    link(dve.tensor_tensor(left[:, :, 2], ge[:, :, 1], ge[:, :, 2], ALU.mult))
                    link(dve.tensor_scalar(s_[7], left, -1.0, 1.0, ALU.mult, ALU.add))
                    dve.wait_ge(top_out[s], nth(i, 2, 2))
                    link(dve.tensor_tensor(s_[8], s_[3], s_[7], ALU.mult))
                    link(dve.tensor_reduce(s1[3], s_[8], AX.X, ALU.add))
                    link(dve.reciprocal(s1[3], s1[3]))
                    link(dve.tensor_tensor(s_[9], s_[8], spread(s1[3]), ALU.mult))
                    yield
                    emptied(("qk", s, 0))
                    x = q01[s][0:HD, :].rearrange("p (b t) -> p b t", t=T)
                    acc = qc[s][0:HD, :].rearrange("p (b t) -> p b t", t=T)
                    link(dve.tensor_scalar(acc, x, ec_w[:, 1:2], ec_b[:, 0:1], ALU.mult, ALU.add))
                    link(dve.scalar_tensor_tensor(out=acc[:, :, 1:T], in0=x[:, :, 0:T - 1], scalar=ec_w[:, 0:1],
                                                  in1=acc[:, :, 1:T], op0=ALU.mult, op1=ALU.add))
                    dve.scalar_tensor_tensor(out=acc[:, :, 0:T - 1], in0=x[:, :, 1:T], scalar=ec_w[:, 2:3],
                                             in1=acc[:, :, 0:T - 1], op0=ALU.mult, op1=ALU.add).then_inc(qc_ready[s], 1)
                    yield
                    yield from attend(s, E, "", 0, HD, s, s_[9])
                    yield
                    residual(("proj", s), s)

                def heads(s):
                    for p in range(2):
                        emptied(("proj", s, p))
                    yield from norm(s, L + 1)
                    for slot in range(5):
                        yield
                    yield from attend(s, H, "1", E, DH, 1)
                    yield
                    residual(("proj1", s), s)

                def mlp(s):
                    for p in range(2):
                        emptied(("proj1", s, p))
                    yield from norm(s, L + 2)
                    for slot in range(4):
                        yield
                    dve.wait_ge(stored, i * (16 * S) + (16 * s + 16))
                    for p in range(2):
                        tile, freed = take(("ffn", s, p))
                        dve.tensor_tensor(result[:, 2 * p:2 * p + 2, :], h[s][:, 2 * p:2 * p + 2, :],
                                          tile[:, 0:2 * C].rearrange("p (b c) -> p b c", b=2), ALU.add).then_inc(freed, 1)
                    yield

                phases(part_, scan, post, norm, before, experts, heads, mlp)
                return links[0] - (0 if part_ == "first" else DVE_LINKS[0])

            first_links = program("first", 0)
            with dve.Fori(0, ROUNDS) as i:
                loop_links = program("loop", i)
            assert (first_links, loop_links) == DVE_LINKS, f"DVE_LINKS = {first_links, loop_links}"


_INS = {
    "ids": "x", "emb": "L0_tok_emb", "norm_w": "L0_tok_norm_w", "in_w": "L0_tok_in_proj_w",
    "conv_w": "L0_tok_conv_w", "conv_b": "L0_tok_conv_b", "x_w": "L0_tok_x_proj_w", "dt_w": "L0_tok_dt_proj_w",
    "dt_b": "L0_tok_dt_proj_b", "A_log": "L0_tok_A_log", "D": "L0_tok_D", "out_w": "L0_tok_out_proj_w",
    "in_w2": "L0_attn_W_in", "conv_w2": "L0_attn_conv_w", "conv_b2": "L0_attn_conv_b", "x_w2": "L0_attn_W_x",
    "dt_w2": "L0_attn_W_dt", "dt_b2": "L0_attn_b_dt", "A_log2": "L0_attn_A_log", "D2": "L0_attn_D",
    "out_w2": "L0_attn_W_out", "Wqk": "L0_ffn_Wqk", "bqk": "L0_ffn_bqk", "Wv": "L0_ffn_Wv", "bv": "L0_ffn_bv",
    "ec_w": "L0_ffn_conv_w", "ec_b": "L0_ffn_conv_b", "Wg1": "L0_ffn_Wg1", "bg1": "L0_ffn_bg1",
    "Wg2": "L0_ffn_Wg2", "bg2": "L0_ffn_bg2", "Wp": "L0_ffn_Wp", "bp": "L0_ffn_bp",
    "Wq": "L1_attn_Wq", "bq": "L1_attn_bq", "Wk": "L1_attn_Wk", "bk": "L1_attn_bk", "Wv1": "L1_attn_Wv",
    "bv1": "L1_attn_bv", "Wo": "L1_attn_Wo", "bo": "L1_attn_bo", "ffn_wi": "L1_ffn_in_weight",
    "ffn_bi": "L1_ffn_in_bias", "ffn_wo": "L1_ffn_out_weight",
}
_TRANSPOSED = ("ids", "ffn_wi")


def kernel(**inputs):
    import numpy as _np
    import concourse.bacc as _bacc
    from concourse import mybir as _mybir
    from concourse.bass_utils import run_bass_kernel_spmd as _run

    nc = _bacc.Bacc("TRN2", target_bir_lowering=False, num_devices=1)
    arrays, A = {}, {}
    for name, given in _INS.items():
        a = _np.asarray(inputs[given])
        a = _np.ascontiguousarray(a.T if name in _TRANSPOSED else a)
        arrays[f"in_{name}_dram"] = a
        A[name] = nc.dram_tensor(f"in_{name}_dram", a.shape, _mybir.dt.from_np(a.dtype), kind="ExternalInput").ap()
    out = nc.dram_tensor("out_0_dram", (128, 128, 192), _mybir.dt.float32, kind="ExternalOutput").ap()
    scratch = nc.dram_tensor("bc_dram", (2, 2, 16, 512), _mybir.dt.float32, kind="Internal").ap()
    tower(nc, A, out, scratch)
    r = _run(nc, [arrays], core_ids=[0])
    return r.results[0]["out_0_dram"]
```
